# Optimizing a Trainium2 kernel written in Bass

```python
import numpy as np
import jax
import jax.numpy as jnp

def _softmax(x, axis=-1):
    return jax.nn.softmax(x, axis=axis)

def _gelu(x):
    return jax.nn.gelu(x, approximate=True)

def _silu(x):
    return jax.nn.silu(x)

def _sigmoid(x):
    return jax.nn.sigmoid(x)

def _layernorm(x, axis=-1, eps=1e-05):
    m = jnp.mean(x, axis=axis, keepdims=True)
    v = jnp.var(x, axis=axis, keepdims=True)
    return (x - m) / jnp.sqrt(v + eps)

def _scatter_add(tgt, idx, src, axis=0):
    return tgt.at[idx].add(src)

def _segment_sum(src, seg, n):
    return jax.ops.segment_sum(src, seg, n)
kernel_name = 'mk_gnn_resnorm_d4_gnn_r64_cc8586'

def setup_inputs(seed: int=0):
    np.random.seed(seed)
    _w = jnp.asarray

    def _rec_inputs():
        import jax
        import jax.numpy as jnp
        _gk = jax.random.key(seed)
        x = -0.0003713 + 1 * jax.random.normal(jax.random.fold_in(_gk, 1), (50000, 128), jnp.float32)
        src = jax.random.randint(jax.random.fold_in(_gk, 2), (25000,), 0, 50000, jnp.int32)
        dst = jax.random.randint(jax.random.fold_in(_gk, 3), (25000,), 0, 50000, jnp.int32)
        _o = jnp.argsort(dst, stable=True)
        src = src[_o]
        dst = dst[_o]
        edge_attr_10 = 0.000254407 + 0.99978 * jax.random.normal(jax.random.fold_in(_gk, 11), (25000, 10), jnp.float32)
        edge_weight = jax.random.uniform(jax.random.fold_in(_gk, 13), (25000,), jnp.float32, 0.0, 0.999998)
        return (x, src, dst, edge_attr_10, edge_weight)
    x, src, dst, edge_attr_10, edge_weight = _rec_inputs()

    def _L0_gnn_setup():
        import jax, jax.numpy as jnp
        import numpy as np
        N_NODES = 100000
        N_EDGES = 25000
        D_IN = 128
        D_HID = 128
        D_OUT = 128

        def sage_conv(x, src, dst, W_l, b_l, W_r, n_nodes):
            msg = x[src]
            agg = jax.ops.segment_sum(msg, dst, num_segments=n_nodes)
            cnt = jax.ops.segment_sum(jnp.ones((src.shape[0],), x.dtype), dst, num_segments=n_nodes)
            mean = agg / jnp.maximum(cnt, 1.0)[:, None]
            return mean @ W_l.T + b_l + x @ W_r.T
        key = jax.random.key(seed)
        ks = jax.random.split(key, 8)
        x = jax.random.normal(ks[0], (N_NODES, D_IN), dtype=jnp.float32)
        edge_index = jax.random.randint(ks[1], (2, N_EDGES), 0, N_NODES, dtype=jnp.int64)
        s1 = 1.0 / np.sqrt(D_IN)
        s2 = 1.0 / np.sqrt(D_HID)
        W1_l = jax.random.uniform(ks[2], (D_HID, D_IN), jnp.float32, -s1, s1)
        b1_l = jax.random.uniform(ks[3], (D_HID,), jnp.float32, -s1, s1)
        W1_r = jax.random.uniform(ks[4], (D_HID, D_IN), jnp.float32, -s1, s1)
        W2_l = jax.random.uniform(ks[5], (D_OUT, D_HID), jnp.float32, -s2, s2)
        b2_l = jax.random.uniform(ks[6], (D_OUT,), jnp.float32, -s2, s2)
        W2_r = jax.random.uniform(ks[7], (D_OUT, D_HID), jnp.float32, -s2, s2)
        return {'x': x, 'edge_index': edge_index, 'W1_l': W1_l, 'b1_l': b1_l, 'W1_r': W1_r, 'W2_l': W2_l, 'b2_l': b2_l, 'W2_r': W2_r}
    _L0_gnn_all = _L0_gnn_setup()
    _L0_gnn_in = {k: v for k, v in _L0_gnn_all.items() if k in ('W1_l', 'b1_l', 'W1_r', 'W2_l', 'b2_l', 'W2_r')}
    del _L0_gnn_all

    def _L1_gnn_setup():
        import jax, jax.numpy as jnp
        import numpy as np
        N = 50000
        E = 12500
        D = 128
        H = 8
        C = D // H
        ED = 10
        FF = 4 * D

        def _layer(x, edge_index, edge_attr, Wq, bq, Wk, bk, Wv, bv, We, Wskip, bskip, Wbeta, gn_w, gn_b, gn_ms, W1, b1, W2, b2):
            n = x.shape[0]
            src, dst = (edge_index[0], edge_index[1])
            q = (x @ Wq + bq).reshape(n, H, C)
            k = (x @ Wk + bk).reshape(n, H, C)
            v = (x @ Wv + bv).reshape(n, H, C)
            e = (edge_attr @ We).reshape(-1, H, C)
            k_j = k[src] + e
            alpha = jnp.einsum('ehc,ehc->eh', q[dst], k_j) / jnp.sqrt(jnp.float32(C))
            amax = jax.ops.segment_max(alpha, dst, num_segments=n)
            ex = jnp.exp(alpha - amax[dst])
            denom = jax.ops.segment_sum(ex, dst, num_segments=n)
            alpha = ex / (denom[dst] + 1e-16)
            msg = (v[src] + e) * alpha[:, :, None]
            out = jax.ops.segment_sum(msg.reshape(-1, H * C), dst, num_segments=n)
            x_r = x @ Wskip + bskip
            beta = jax.nn.sigmoid(jnp.concatenate([out, x_r, out - x_r], axis=-1) @ Wbeta)
            x_att = beta * x_r + (1.0 - beta) * out
            h = x + x_att
            mean = h.mean(axis=0)
            hc = h - gn_ms * mean
            var = (hc * hc).mean(axis=0)
            h = hc / jnp.sqrt(var + 1e-05) * gn_w + gn_b
            ffn = jax.nn.gelu(h @ W1 + b1, approximate=False) @ W2 + b2
            return h + ffn
        key = jax.random.key(seed)
        ks = jax.random.split(key, 20)
        s = 0.05
        p = lambda k, shape: jax.random.normal(k, shape, jnp.float32) * s
        return {'x': jax.random.normal(ks[0], (N, D), jnp.float32), 'edge_index': jax.random.randint(ks[1], (2, E), 0, N), 'edge_attr': jax.random.normal(ks[2], (E, ED), jnp.float32), 'Wq': p(ks[3], (D, D)), 'bq': jnp.zeros((D,), jnp.float32), 'Wk': p(ks[4], (D, D)), 'bk': jnp.zeros((D,), jnp.float32), 'Wv': p(ks[5], (D, D)), 'bv': jnp.zeros((D,), jnp.float32), 'We': p(ks[6], (ED, D)), 'Wskip': p(ks[7], (D, D)), 'bskip': jnp.zeros((D,), jnp.float32), 'Wbeta': p(ks[8], (3 * D, 1)), 'gn_w': jnp.ones((D,), jnp.float32), 'gn_b': jnp.zeros((D,), jnp.float32), 'gn_ms': jnp.ones((D,), jnp.float32), 'W1': p(ks[9], (D, FF)), 'b1': jnp.zeros((FF,), jnp.float32), 'W2': p(ks[10], (FF, D)), 'b2': jnp.zeros((D,), jnp.float32)}
    _L1_gnn_all = _L1_gnn_setup()
    _L1_gnn_in = {k: v for k, v in _L1_gnn_all.items() if k in ('Wq', 'bq', 'Wk', 'bk', 'Wv', 'bv', 'We', 'Wskip', 'bskip', 'Wbeta', 'gn_w', 'gn_b', 'gn_ms', 'W1', 'b1', 'W2', 'b2')}
    del _L1_gnn_all

    def _L2_gnn_setup():
        import jax, jax.numpy as jnp
        import numpy as np
        N, E = (50000, 12500)
        IN, HID, OUT = (128, 256, 128)
        BN_EPS = 1e-05
        key = jax.random.key(seed)
        ks = jax.random.split(key, 12)
        x = jax.random.normal(ks[0], (N, IN), dtype=jnp.float32)
        edge_index = jax.random.randint(ks[1], (2, E), 0, N, dtype=jnp.int64)
        edge_weight = jax.random.uniform(ks[2], (E,), dtype=jnp.float32)
        W0 = jax.random.normal(ks[3], (IN, HID), dtype=jnp.float32) * (1.0 / np.sqrt(IN))
        b0 = jnp.zeros((HID,), jnp.float32)
        W1 = jax.random.normal(ks[4], (HID, HID), dtype=jnp.float32) * (1.0 / np.sqrt(HID))
        b1 = jnp.zeros((HID,), jnp.float32)
        Wl = jax.random.normal(ks[5], (HID, OUT), dtype=jnp.float32) * (1.0 / np.sqrt(HID))
        bl = jnp.zeros((OUT,), jnp.float32)
        g0 = 1.0 + 0.1 * jax.random.normal(ks[6], (HID,), dtype=jnp.float32)
        be0 = 0.1 * jax.random.normal(ks[7], (HID,), dtype=jnp.float32)
        g1 = 1.0 + 0.1 * jax.random.normal(ks[8], (HID,), dtype=jnp.float32)
        be1 = 0.1 * jax.random.normal(ks[9], (HID,), dtype=jnp.float32)
        return {'x': x, 'edge_index': edge_index, 'edge_weight': edge_weight, 'W0': W0, 'b0': b0, 'W1': W1, 'b1': b1, 'Wl': Wl, 'bl': bl, 'g0': g0, 'be0': be0, 'g1': g1, 'be1': be1}
    _L2_gnn_all = _L2_gnn_setup()
    _L2_gnn_in = {k: v for k, v in _L2_gnn_all.items() if k in ('W0', 'b0', 'W1', 'b1', 'Wl', 'bl', 'g0', 'be0', 'g1', 'be1')}
    del _L2_gnn_all

    def _L3_gnn_setup():
        import jax, jax.numpy as jnp
        import numpy as np
        N_NODES = 100000
        N_EDGES = 10000
        IN_DIM = 128
        OUT_DIM = 128
        key = jax.random.key(seed)
        k1, k2, k3 = jax.random.split(key, 3)
        node_features = jax.random.normal(k1, (N_NODES, IN_DIM), dtype=jnp.float32)
        edge_index = jax.random.randint(k2, (2, N_EDGES), 0, N_NODES, dtype=jnp.int64)
        W = jax.random.normal(k3, (IN_DIM, OUT_DIM), dtype=jnp.float32) / np.sqrt(IN_DIM).astype(np.float32)
        b = jnp.zeros((OUT_DIM,), dtype=jnp.float32)
        return {'node_features': node_features, 'edge_index': edge_index, 'W': W, 'b': b}
    _L3_gnn_all = _L3_gnn_setup()
    _L3_gnn_in = {k: v for k, v in _L3_gnn_all.items() if k in ('W', 'b')}
    del _L3_gnn_all
    return {'x': x, 'src': src, 'dst': dst, 'edge_attr_10': edge_attr_10, 'edge_weight': edge_weight, 'L0_gnn_W1_l': _L0_gnn_in['W1_l'], 'L0_gnn_b1_l': _L0_gnn_in['b1_l'], 'L0_gnn_W1_r': _L0_gnn_in['W1_r'], 'L0_gnn_W2_l': _L0_gnn_in['W2_l'], 'L0_gnn_b2_l': _L0_gnn_in['b2_l'], 'L0_gnn_W2_r': _L0_gnn_in['W2_r'], 'L1_gnn_Wq': _L1_gnn_in['Wq'], 'L1_gnn_bq': _L1_gnn_in['bq'], 'L1_gnn_Wk': _L1_gnn_in['Wk'], 'L1_gnn_bk': _L1_gnn_in['bk'], 'L1_gnn_Wv': _L1_gnn_in['Wv'], 'L1_gnn_bv': _L1_gnn_in['bv'], 'L1_gnn_We': _L1_gnn_in['We'], 'L1_gnn_Wskip': _L1_gnn_in['Wskip'], 'L1_gnn_bskip': _L1_gnn_in['bskip'], 'L1_gnn_Wbeta': _L1_gnn_in['Wbeta'], 'L1_gnn_gn_w': _L1_gnn_in['gn_w'], 'L1_gnn_gn_b': _L1_gnn_in['gn_b'], 'L1_gnn_gn_ms': _L1_gnn_in['gn_ms'], 'L1_gnn_W1': _L1_gnn_in['W1'], 'L1_gnn_b1': _L1_gnn_in['b1'], 'L1_gnn_W2': _L1_gnn_in['W2'], 'L1_gnn_b2': _L1_gnn_in['b2'], 'L2_gnn_W0': _L2_gnn_in['W0'], 'L2_gnn_b0': _L2_gnn_in['b0'], 'L2_gnn_W1': _L2_gnn_in['W1'], 'L2_gnn_b1': _L2_gnn_in['b1'], 'L2_gnn_Wl': _L2_gnn_in['Wl'], 'L2_gnn_bl': _L2_gnn_in['bl'], 'L2_gnn_g0': _L2_gnn_in['g0'], 'L2_gnn_be0': _L2_gnn_in['be0'], 'L2_gnn_g1': _L2_gnn_in['g1'], 'L2_gnn_be1': _L2_gnn_in['be1'], 'L3_gnn_W': _L3_gnn_in['W'], 'L3_gnn_b': _L3_gnn_in['b']}

def reference(x, src, dst, edge_attr_10, edge_weight, L0_gnn_W1_l, L0_gnn_b1_l, L0_gnn_W1_r, L0_gnn_W2_l, L0_gnn_b2_l, L0_gnn_W2_r, L1_gnn_Wq, L1_gnn_bq, L1_gnn_Wk, L1_gnn_bk, L1_gnn_Wv, L1_gnn_bv, L1_gnn_We, L1_gnn_Wskip, L1_gnn_bskip, L1_gnn_Wbeta, L1_gnn_gn_w, L1_gnn_gn_b, L1_gnn_gn_ms, L1_gnn_W1, L1_gnn_b1, L1_gnn_W2, L1_gnn_b2, L2_gnn_W0, L2_gnn_b0, L2_gnn_W1, L2_gnn_b1, L2_gnn_Wl, L2_gnn_bl, L2_gnn_g0, L2_gnn_be0, L2_gnn_g1, L2_gnn_be1, L3_gnn_W, L3_gnn_b):
    import jax
    import jax.numpy as jnp

    def _L0_gnn_ref(x, edge_index, W1_l, b1_l, W1_r, W2_l, b2_l, W2_r):
        import jax, jax.numpy as jnp
        import numpy as np
        N_NODES = 100000
        N_EDGES = 25000
        D_IN = 128
        D_HID = 128
        D_OUT = 128

        def sage_conv(x, src, dst, W_l, b_l, W_r, n_nodes):
            msg = x[src]
            agg = jax.ops.segment_sum(msg, dst, num_segments=n_nodes)
            cnt = jax.ops.segment_sum(jnp.ones((src.shape[0],), x.dtype), dst, num_segments=n_nodes)
            mean = agg / jnp.maximum(cnt, 1.0)[:, None]
            return mean @ W_l.T + b_l + x @ W_r.T
        src, dst = (edge_index[0], edge_index[1])
        n = x.shape[0]
        h = sage_conv(x, src, dst, W1_l, b1_l, W1_r, n)
        h = jax.nn.relu(h)
        out = sage_conv(h, src, dst, W2_l, b2_l, W2_r, n)
        return out

    def _L1_gnn_ref(x, edge_index, edge_attr, Wq, bq, Wk, bk, Wv, bv, We, Wskip, bskip, Wbeta, gn_w, gn_b, gn_ms, W1, b1, W2, b2):
        import jax, jax.numpy as jnp
        import numpy as np
        N = 50000
        E = 12500
        D = 128
        H = 8
        C = D // H
        ED = 10
        FF = 4 * D

        def _layer(x, edge_index, edge_attr, Wq, bq, Wk, bk, Wv, bv, We, Wskip, bskip, Wbeta, gn_w, gn_b, gn_ms, W1, b1, W2, b2):
            n = x.shape[0]
            src, dst = (edge_index[0], edge_index[1])
            q = (x @ Wq + bq).reshape(n, H, C)
            k = (x @ Wk + bk).reshape(n, H, C)
            v = (x @ Wv + bv).reshape(n, H, C)
            e = (edge_attr @ We).reshape(-1, H, C)
            k_j = k[src] + e
            alpha = jnp.einsum('ehc,ehc->eh', q[dst], k_j) / jnp.sqrt(jnp.float32(C))
            amax = jax.ops.segment_max(alpha, dst, num_segments=n)
            ex = jnp.exp(alpha - amax[dst])
            denom = jax.ops.segment_sum(ex, dst, num_segments=n)
            alpha = ex / (denom[dst] + 1e-16)
            msg = (v[src] + e) * alpha[:, :, None]
            out = jax.ops.segment_sum(msg.reshape(-1, H * C), dst, num_segments=n)
            x_r = x @ Wskip + bskip
            beta = jax.nn.sigmoid(jnp.concatenate([out, x_r, out - x_r], axis=-1) @ Wbeta)
            x_att = beta * x_r + (1.0 - beta) * out
            h = x + x_att
            mean = h.mean(axis=0)
            hc = h - gn_ms * mean
            var = (hc * hc).mean(axis=0)
            h = hc / jnp.sqrt(var + 1e-05) * gn_w + gn_b
            ffn = jax.nn.gelu(h @ W1 + b1, approximate=False) @ W2 + b2
            return h + ffn
        return _layer(x, edge_index, edge_attr, Wq, bq, Wk, bk, Wv, bv, We, Wskip, bskip, Wbeta, gn_w, gn_b, gn_ms, W1, b1, W2, b2)

    def _L2_gnn_ref(x, edge_index, edge_weight, W0, b0, W1, b1, Wl, bl, g0, be0, g1, be1):
        import jax, jax.numpy as jnp
        import numpy as np
        N, E = (50000, 12500)
        IN, HID, OUT = (128, 256, 128)
        BN_EPS = 1e-05
        n = x.shape[0]
        row, col = (edge_index[0], edge_index[1])
        ar = jnp.arange(n)
        rowf = jnp.concatenate([row, ar])
        colf = jnp.concatenate([col, ar])
        wf = jnp.concatenate([edge_weight, jnp.ones((n,), x.dtype)])
        deg = jax.ops.segment_sum(wf, colf, num_segments=n)
        dinv = jnp.where(deg > 0, jax.lax.rsqrt(deg), 0.0)
        norm = dinv[rowf] * wf * dinv[colf]

        def conv(h, W, b):
            h = h @ W
            msg = h[rowf] * norm[:, None]
            return jax.ops.segment_sum(msg, colf, num_segments=n) + b

        def bn_eval(h, g, b):
            return h * (g / jnp.sqrt(1.0 + BN_EPS)) + b
        h = jax.nn.relu(bn_eval(conv(x, W0, b0), g0, be0))
        h = jax.nn.relu(bn_eval(conv(h, W1, b1), g1, be1))
        h = conv(h, Wl, bl)
        return jax.nn.log_softmax(h, axis=1)

    def _L3_gnn_ref(node_features, edge_index, W, b):
        import jax, jax.numpy as jnp
        import numpy as np
        N_NODES = 100000
        N_EDGES = 10000
        IN_DIM = 128
        OUT_DIM = 128
        src, dst = (edge_index[0], edge_index[1])
        n = node_features.shape[0]
        agg = jax.ops.segment_sum(node_features[src], dst, num_segments=n)
        deg = jax.ops.segment_sum(jnp.ones_like(dst, dtype=node_features.dtype), dst, num_segments=n)
        deg = jnp.maximum(deg, 1.0)[:, None]
        pooled = agg / deg
        return jax.nn.relu(pooled @ W + b)
    edge_index = jnp.stack([src, dst])
    x = _layernorm(x + _L0_gnn_ref(x, edge_index, L0_gnn_W1_l, L0_gnn_b1_l, L0_gnn_W1_r, L0_gnn_W2_l, L0_gnn_b2_l, L0_gnn_W2_r), axis=-1)
    x = _layernorm(x + _L1_gnn_ref(x, edge_index, edge_attr_10, L1_gnn_Wq, L1_gnn_bq, L1_gnn_Wk, L1_gnn_bk, L1_gnn_Wv, L1_gnn_bv, L1_gnn_We, L1_gnn_Wskip, L1_gnn_bskip, L1_gnn_Wbeta, L1_gnn_gn_w, L1_gnn_gn_b, L1_gnn_gn_ms, L1_gnn_W1, L1_gnn_b1, L1_gnn_W2, L1_gnn_b2), axis=-1)
    x = _layernorm(x + _L2_gnn_ref(x, edge_index, edge_weight, L2_gnn_W0, L2_gnn_b0, L2_gnn_W1, L2_gnn_b1, L2_gnn_Wl, L2_gnn_bl, L2_gnn_g0, L2_gnn_be0, L2_gnn_g1, L2_gnn_be1), axis=-1)
    x = _layernorm(x + _L3_gnn_ref(x, edge_index, L3_gnn_W, L3_gnn_b), axis=-1)
    return x

_drawn_inputs = setup_inputs


def setup_inputs(seed=0):
    import zlib

    import numpy as np

    out = dict(_drawn_inputs(seed))
    spreads = {'L1_gnn_bq': (0.0, 0.8),
     'L1_gnn_bk': (0.0, 0.8),
     'L1_gnn_bv': (0.0, 0.618),
     'L1_gnn_bskip': (0.0, 0.8),
     'L1_gnn_gn_w': (1.0, 0.2),
     'L1_gnn_gn_b': (0.0, 0.1),
     'L1_gnn_gn_ms': (1.0, 0.6),
     'L1_gnn_b1': (0.0, 0.1),
     'L1_gnn_b2': (0.0, 0.1),
     'L2_gnn_b0': (0.0, 0.1),
     'L2_gnn_b1': (0.0, 0.1),
     'L2_gnn_bl': (0.0, 0.1),
     'L3_gnn_b': (0.0, 0.1)}
    factors = {'L0_gnn_b1_l': 3.224, 'L1_gnn_Wq': 8.0, 'L1_gnn_Wk': 8.0}
    for name, (base, spread) in spreads.items():
        noise = np.random.default_rng([zlib.crc32(name.encode()), seed]).standard_normal(out[name].shape)
        drawn = base * np.exp(spread * noise) if base else spread * noise
        out[name] = jnp.asarray(drawn.astype(out[name].dtype))
    for name, factor in factors.items():
        out[name] = (out[name] * factor).astype(out[name].dtype)
    return out
```

```python
import concourse.bass as bass
from concourse import mybir
from contextlib import ExitStack

F32 = mybir.dt.float32
BF16 = mybir.dt.bfloat16
I32 = mybir.dt.int32
ALU = mybir.AluOpType
ACT = mybir.ActivationFunctionType
AX = mybir.AxisListType

P = 128
D = 128
N_NODES, N_EDGES = 50000, 25000
NB = 4
TILE = NB * P
TILES = -(-N_NODES // TILE)
NODES = TILES * TILE
LAST = N_NODES - (TILES - 1) * TILE
EB = -(-N_EDGES // P)
EDGES = EB * P
EROWS = EDGES + P
GB = 7
BATCHES = EB // GB
EBATCH = 4
ETILE = EBATCH * P
ETILES = EB // EBATCH
U = 3
STEPS = 304
META = 8
HEADS, HC = 8, 16
HID = 256
FF = 512
BIG = 3.0e38
EPS = 1e-5
BROW = {"b1l": (0, 128), "b2l": (128, 128), "skip": (256, 129), "ffn2": (388, 128),
        "pool": (516, 128), "gcn0": (644, 256), "gcn1": (900, 256)}
BROWS = 1156


class Names(dict):

    def __getattr__(self, name):
        return self[name]

    def __setattr__(self, name, value):
        self[name] = value


def ds(a, n):
    return bass.ds(a, n)


def rows_at(dram, node):
    return dram[ds(node, TILE), :].rearrange("(b p) f -> p b f", p=P)


def rows_tile(dram, t):
    return rows_at(dram, t * TILE)


class Chain:

    def __init__(self, eng, sem, per):
        self.eng, self.sem, self.per = eng, sem, per

    def begin(self, step):
        self.base, self.n = step * self.per, 0

    def resume(self, step, n):
        self.base, self.n = step * self.per, n

    def link(self, ins):
        self.n += 1
        assert self.n <= self.per
        ins.then_inc(self.sem, 1)
        self.eng.wait_ge(self.sem, self.base + self.n)

    def mark(self, ins):
        self.n += 1
        assert self.n <= self.per
        ins.then_inc(self.sem, 1)


def row_variance(V, chain, stats, work, var_eps):
    V.tensor_tensor(work[:, :, 0], stats[:, :, 1], stats[:, :, 4], ALU.add)
    V.scalar_tensor_tensor(work[:, :, 2], stats[:, :, 2], D * EPS, stats[:, :, 5], ALU.add, ALU.add)
    chain.link(V.tensor_tensor(work[:, :, 1], stats[:, :, 1], stats[:, :, 4], ALU.subtract))
    chain.link(V.scalar_tensor_tensor(work[:, :, 1], work[:, :, 1], 0.25, work[:, :, 1], ALU.mult, ALU.mult))
    chain.mark(V.scalar_tensor_tensor(var_eps, work[:, :, 2], 1.0 / D, work[:, :, 1], ALU.mult, ALU.add))


def setup_phase(nc, C, A):
    ctx = ExitStack()
    with ctx:
        def sb(name, shape, dt=F32):
            return ctx.enter_context(nc.sbuf_tensor("p0_" + name, shape, dt))

        def sem(name):
            C.sems.append(ctx.enter_context(nc.semaphore("p0_" + name)))
            return C.sems[-1]

        dst_i = sb("dst_i", [P, EB], I32)
        tau_i = sb("tau_i", [P, EB], I32)
        blk_i = sb("blk_i", [P, EB], I32)
        tau_f = sb("tau_f", [P, EB])
        blk_f = sb("blk_f", [P, EB])
        oh_t = sb("oh_t", [P, 28, TILES], BF16)
        oh_b = sb("oh_b", [P, EB, NB], BF16)
        iota_i = sb("iota_i", [P, TILE], I32)
        pidx_i = sb("pidx_i", [P, 1], I32)
        pidx = sb("pidx", [P, 1])
        head_i = sb("head_i", [P, 1], I32)
        head_f = sb("head_f", [P, 1])
        cnt = sb("cnt", [TILES, NB])
        ceil_f = sb("ceil_f", [TILES, NB])
        ceil_i = sb("ceil_i", [TILES, NB], I32)
        ceil_j = sb("ceil_j", [TILES, NB], I32)
        rt = sb("rt", [TILES, 2])
        upper = sb("upper", [TILES, TILES])
        quant = sb("quant", [TILES, 7])
        endc = sb("endc", [TILES, 1])
        sel = sb("sel", [TILES, STEPS])
        sel2 = sb("sel2", [TILES, STEPS])
        bc = sb("bc", [TILES, 2, P])
        onesf = sb("onesf", [P, P])
        minus1 = sb("minus1", [P, 131])
        zrow = sb("zrow", [P, HID])
        quant_sb = sb("quant_sb", [7, STEPS])
        row = sb("row", [1, 7, STEPS])
        dummy = sb("dummy", [1, STEPS])
        rnd = sb("rnd", [1, STEPS])
        rnd2 = sb("rnd2", [1, STEPS])
        tmp = sb("tmp", [1, STEPS])
        need_i = sb("need_i", [1, STEPS], I32)
        need_e = sb("need_e", [1, STEPS], I32)
        srow = sb("srow", [1, 2])
        trips_f = sb("trips_f", [1, 1])
        w_sb = sb("w_sb", [P, EB])
        brow = sb("brow", [1, BROWS])
        brow2 = sb("brow2", [1, 4, HID])
        bsplit = sb("bsplit", [1, 3, BROWS], BF16)
        wbc = sb("wbc", [P, 2, D])
        wcols = sb("wcols", [P, 2])
        dcol = sb("dcol", [P, 1])
        bskc = sb("bskc", [P, 1])
        wskT = sb("wskT", [P, D])
        gbc = sb("gbc", [P, 2, HID])
        tmpk = sb("tmpk", [P, STEPS])
        pcnt = ctx.enter_context(nc.psum_tensor("p0_pcnt", [TILES, NB], F32))
        ppre = ctx.enter_context(nc.psum_tensor("p0_ppre", [TILES, 2], F32))
        psel = ctx.enter_context(nc.psum_tensor("p0_psel", [7, STEPS], F32))
        pst = ctx.enter_context(nc.psum_tensor("p0_pst", [P, STEPS], F32))
        pta = ctx.enter_context(nc.psum_tensor("p0_pta", [P, STEPS], F32))
        psum1 = ctx.enter_context(nc.psum_tensor("p0_psum1", [1, 2], F32))
        pu = ctx.enter_context(nc.psum_tensor("p0_pu", [P, 2], F32))

        loaded_dst, loaded_w, loaded_c = sem("loaded_dst"), sem("loaded_w"), sem("loaded_c")
        made = sem("made")
        dve_made = sem("dve_made")
        block_oh, rounds_ready, sel_ready = sem("block_oh"), sem("rounds_ready"), sem("sel_ready")
        quant_ready, dcol_ready, split_ready = sem("quant_ready"), sem("dcol_ready"), sem("split_ready")
        oh_made = sem("oh_made")
        oh_used = sem("oh_used")
        pe_made = sem("pe_made")
        bounced = sem("bounced")
        row_in = sem("row_in")
        zeroed = sem("zeroed")
        split_in = sem("split_in")
        block = ctx.enter_context(nc.Block())
        GRP = 28
        NG = EB // GRP

        @block.sync
        def _(sp):
            sp.dma_start(dst_i[:, :], A.dst_cols).then_inc(loaded_dst, 16)
            for dst, src in (
                (C.src_sb[:, :], A.src_cols), (C.dst_sb[:, :], A.dst_cols),
                (C.w1l[:, :], A.W1lT), (C.w1r[:, :], A.W1rT), (C.w2l[:, :], A.W2lT), (C.w2r[:, :], A.W2rT),
                (C.wq[:, :], A.Wq), (C.wk[:, :], A.Wk), (C.wv[:, :], A.Wv),
                (C.wek[0:10, :], A.We), (C.wek[10:11, :], A.bk), (C.wev[0:10, :], A.We), (C.wev[10:11, :], A.bv),
                (C.bq[:, :], A.bq), (C.wsk[:, 0:D], A.Wskip), (wskT[:, :], A.WskipT),
                (C.gnw[:, :], A.gn_w), (C.gnb[:, :], A.gn_b), (C.gnms[:, :], A.gn_ms),
                (C.wf1[:, :], A.fW1), (C.bf1[:, :], A.fb1),
                (C.wf2[:, :, :], A.fW2.rearrange("(c p) o -> p c o", p=P)),
                (C.wg0[:, :], A.gW0), (C.wg1[:, :, :], A.gW1.rearrange("(c p) o -> p c o", p=P)),
                (C.wgl[:, :, :], A.gWl.rearrange("(c p) o -> p c o", p=P)),
                (C.wp[:, :], A.pW), (C.bl_bc[:, :], A.gbl.partition_broadcast(P)[:, 0, :]),
            ):
                sp.dma_start(dst, src).then_inc(loaded_w, 16)
            C.n_w = 27
            sp.dma_start(w_sb[:, :], A.w_cols).then_inc(loaded_c, 16)
            for name, src in (("b1l", A.b1l), ("b2l", A.b2l), ("skip", A.bskip), ("ffn2", A.fb2), ("pool", A.pb)):
                at = BROW[name][0]
                sp.dma_start(brow[:, at:at + D], src).then_inc(loaded_c, 16)
            for n, src in enumerate((A.gb0, A.gb1, A.gbe0, A.gbe1)):
                sp.dma_start(brow2[:, n, :], src).then_inc(loaded_c, 16)
            sp.dma_start(gbc[:, 0, :], A.gg0.partition_broadcast(P)[:, 0, :]).then_inc(loaded_c, 16)
            sp.dma_start(gbc[:, 1, :], A.gg1.partition_broadcast(P)[:, 0, :]).then_inc(loaded_c, 16)
            sp.dma_start(wbc[:, 0, :], A.wbeta_a.partition_broadcast(P)[:, 0, :]).then_inc(loaded_c, 16)
            sp.dma_start(wbc[:, 1, :], A.wbeta_c.partition_broadcast(P)[:, 0, :]).then_inc(loaded_c, 16)
            sp.dma_start(wcols[:, 0:1], A.wbeta_b_col).then_inc(loaded_c, 16)
            sp.dma_start(wcols[:, 1:2], A.wbeta_c_col).then_inc(loaded_c, 16)
            sp.dma_start(bskc[:, :], A.bskip_col).then_inc(loaded_c, 16)
            sp.wait_ge(made, 7)
            for m, w in ((C.msg, D), (C.msga, D + HEADS), (C.msg2, HID)):
                sp.dma_start(m[EDGES:EROWS, :], zrow[:, 0:w]).then_inc(zeroed, 16)
            sp.dma_start(C.msgx[EDGES:EROWS, :], minus1[:, :]).then_inc(zeroed, 16)
            sp.wait_ge(quant_ready, 1)
            sp.dma_start(C.bounce[:, :], quant_sb[:, :]).then_inc(bounced, 16)
            sp.wait_ge(bounced, 16)
            sp.dma_start(row[:, :, :], C.bounce[:, :].rearrange("(o q) s -> o q s", o=1)).then_inc(row_in, 16)
            sp.wait_ge(split_ready, 1)
            for n in range(3):
                sp.dma_start(C.bias3[n:n + 1, :], bsplit[:, n, :]).then_inc(split_in, 16)
            sp.wait_ge(split_in, 48)
            sp.wait_ge(loaded_w, 16 * C.n_w)
            sp.wait_ge(zeroed, 64)

        @block.gpsimd
        def _(pool):
            nc.gpsimd.iota(iota_i[:, :], pattern=[[1, TILE]], base=0, channel_multiplier=0).then_inc(made, 1)
            nc.gpsimd.iota(pidx_i[:, :], pattern=[[0, 1]], base=0, channel_multiplier=1).then_inc(made, 1)
            nc.gpsimd.memset(C.ident[:, :], 0.0).then_inc(made, 1)
            nc.gpsimd.memset(onesf[:, :], 1.0).then_inc(made, 1)
            nc.gpsimd.memset(zrow[:, :], 0.0).then_inc(made, 1)
            nc.gpsimd.memset(minus1[:, :], -1.0).then_inc(made, 1)
            nc.gpsimd.memset(C.gate[:, :], 1.0).then_inc(made, 1)
            pool.wait_ge(made, 7)
            pool.affine_select(out=C.ident[:, :], in_=C.ident[:, :], compare_op=ALU.not_equal, fill=1.0,
                               base=0, pattern=[[-1, P]], channel_multiplier=1).then_inc(made, 1)
            nc.gpsimd.memset(C.ones3[:, :], 1.0).then_inc(made, 1)
            nc.gpsimd.memset(C.ext[:, :, 0:1], 1.0).then_inc(made, 1)

        @block.vector
        def _(dve):
            V = nc.vector
            chain = Chain(dve, dve_made, 999)
            chain.begin(0)
            L = chain.link
            dve.wait_ge(loaded_dst, 16)
            L(V.tensor_scalar(tau_i[:, :], dst_i[:, :], 9, None, ALU.logical_shift_right))
            L(V.tensor_scalar(blk_i[:, :], dst_i[:, :], 7, 3, ALU.logical_shift_right, ALU.bitwise_and))
            L(V.tensor_copy(tau_f[:, :], tau_i[:, :]))
            L(V.tensor_copy(blk_f[:, :], blk_i[:, :]))
            dve.wait_ge(made, 10)
            L(V.tensor_copy(C.iota[:, :], iota_i[:, :]))
            L(V.tensor_copy(pidx[:, :], pidx_i[:, :]))
            L(V.tensor_tensor(oh_b[:, :, :], C.iota[:, 0:NB].unsqueeze(1).to_broadcast([P, EB, NB]),
                              blk_f[:, :].unsqueeze(2).to_broadcast([P, EB, NB]), ALU.is_equal))
            dve.sem_inc(block_oh, 1)
            for g in range(NG):
                if g:
                    dve.wait_ge(oh_used, g)
                V.tensor_tensor(oh_t[:, :, :], C.iota[:, 0:TILES].unsqueeze(1).to_broadcast([P, GRP, TILES]),
                                tau_f[:, g * GRP:(g + 1) * GRP].unsqueeze(2).to_broadcast([P, GRP, TILES]),
                                ALU.is_equal).then_inc(oh_made, 1)
            dve.wait_ge(oh_used, NG)
            L(V.tensor_copy(cnt[:, :], pcnt[:, :]))
            L(V.tensor_scalar(ceil_i[:, :], cnt[:, :], float(P - 1), None, ALU.add))
            L(V.tensor_scalar(ceil_j[:, :], ceil_i[:, :], 7, None, ALU.logical_shift_right))
            L(V.tensor_copy(ceil_f[:, :], ceil_j[:, :]))
            L(V.tensor_reduce(rt[:, 0:1], ceil_f[:, :], AX.X, ALU.max))
            L(V.tensor_scalar(rt[:, 0:1], rt[:, 0:1], 1.0, None, ALU.max))
            L(V.tensor_reduce(rt[:, 1:2], cnt[:, :], AX.X, ALU.add))
            L(V.tensor_scalar(upper[:, :], C.iota[0:TILES, 0:TILES], pidx[0:TILES, :], None, ALU.is_gt))
            dve.sem_inc(rounds_ready, 1)
            dve.wait_ge(pe_made, 1)
            L(V.tensor_copy(quant[:, 1:3], ppre[:, :]))
            L(V.tensor_copy(quant[:, 0:1], pidx[0:TILES, :]))
            L(V.memset(quant[:, 6:7], 1.0))
            for b in range(1, NB):
                L(V.tensor_tensor(quant[:, 2 + b:3 + b], quant[:, 1 + b:2 + b], cnt[:, b - 1:b], ALU.add))
            L(V.tensor_tensor(endc[:, :], quant[:, 1:2], rt[:, 0:1], ALU.add))
            L(V.tensor_scalar(sel2[:, :], C.iota[0:TILES, 0:STEPS], endc[:, :], None, ALU.is_lt))
            L(V.tensor_copy(bc[:, 0, :], quant[:, 1:2].to_broadcast([TILES, P])))
            L(V.tensor_copy(bc[:, 1, :], quant[:, 0:1].to_broadcast([TILES, P])))
            L(V.scalar_tensor_tensor(sel[:, :], C.iota[0:TILES, 0:STEPS], quant[:, 1:2], sel2[:, :],
                                     ALU.is_ge, ALU.mult))
            dve.sem_inc(sel_ready, 1)
            dve.wait_ge(pe_made, 2)
            L(V.tensor_copy(quant_sb[:, :], psel[:, :]))
            dve.sem_inc(quant_ready, 1)
            L(V.tensor_tensor(tmpk[:, :], C.iota[:, 0:STEPS], pst[:, :], ALU.subtract))
            L(V.tensor_scalar(C.keep[:, :], tmpk[:, :], 0.0, None, ALU.is_gt))
            L(V.tensor_scalar(C.base[:, :], pta[:, :], float(TILE), None, ALU.mult))
            L(V.tensor_copy(srow[:, :], psum1[:, :]))
            L(V.tensor_scalar(srow[:, 0:1], srow[:, 0:1], float(U - 1), None, ALU.add))
            L(V.tensor_scalar(tmp[:, :], C.iota[0:1, 0:STEPS], float(U), srow[:, 0:1], ALU.mult, ALU.is_le))
            L(V.tensor_reduce(trips_f[:, :], tmp[:, :], AX.X, ALU.add))
            L(V.tensor_scalar(C.trips[:, 0:1], trips_f[:, :], 1.0, None, ALU.subtract))
            L(V.tensor_scalar(C.trips[:, 1:2], trips_f[:, :], 2.0, None, ALU.subtract))
            dve.wait_ge(row_in, 16)
            meta = C.meta[:, :].rearrange("o (s c) -> o s c", c=META)
            L(V.tensor_scalar(dummy[:, :], row[:, 6, :], -1.0, 1.0, ALU.mult, ALU.add))
            L(V.tensor_tensor(rnd[:, :], C.iota[0:1, 0:STEPS], row[:, 1, :], ALU.subtract))
            L(V.scalar_tensor_tensor(rnd2[:, :], dummy[:, :], float(TILES - 1), row[:, 0, :], ALU.mult, ALU.add))
            L(V.tensor_copy(meta[:, :, 7], rnd2[:, :]))
            L(V.tensor_scalar(meta[:, :, 4], rnd2[:, :], float(TILE), None, ALU.mult))
            L(V.tensor_scalar(rnd[:, :], rnd[:, :], float(P), None, ALU.mult))
            L(V.scalar_tensor_tensor(rnd[:, :], dummy[:, :], float(EDGES), rnd[:, :], ALU.mult, ALU.add))
            for b in range(NB):
                L(V.tensor_tensor(tmp[:, :], row[:, 2 + b, :], rnd[:, :], ALU.add))
                L(V.tensor_scalar(meta[:, :, b], tmp[:, :], float(EDGES), None, ALU.min))
            L(V.tensor_scalar(tmp[:, :], tmp[:, :], float(EDGES), None, ALU.min))
            L(V.tensor_scalar(tmp[:, :], tmp[:, :], 1.0 / (GB * P), (P - 1.0) / (GB * P) + 1.01, ALU.mult, ALU.add))
            L(V.tensor_scalar(need_i[:, :], tmp[:, :], 2.0, float(BATCHES), ALU.max, ALU.min))
            L(V.tensor_scalar(need_e[:, :], need_i[:, :], 1, None, ALU.logical_shift_right))
            L(V.tensor_scalar(meta[:, :, 6], need_e[:, :], 16.0, None, ALU.mult))
            L(V.tensor_scalar(need_i[:, :], need_i[:, :], 1.0, None, ALU.add))
            L(V.tensor_scalar(need_e[:, :], need_i[:, :], 1, None, ALU.logical_shift_right))
            L(V.tensor_scalar(meta[:, :, 5], need_e[:, :], 16.0, None, ALU.mult))
            dve.wait_ge(loaded_c, 16 * 17)
            dve.wait_ge(loaded_w, 16 * C.n_w)
            inv = float((1.0 + EPS) ** -0.5)
            for n, name in enumerate(("gcn0", "gcn1")):
                at = BROW[name][0]
                b2 = brow[:, at:at + HID]
                L(V.scalar_tensor_tensor(b2, gbc[0:1, n, :], inv, brow2[:, n, :], ALU.mult, ALU.mult))
                L(V.tensor_tensor(b2, b2, brow2[:, 2 + n, :], ALU.add))
            L(V.scalar_tensor_tensor(C.wg0[:, :], gbc[:, 0, :], inv, C.wg0[:, :], ALU.mult, ALU.mult))
            for c in range(2):
                L(V.scalar_tensor_tensor(C.wg1[:, c, :], gbc[:, 1, :], inv, C.wg1[:, c, :], ALU.mult, ALU.mult))
            L(V.tensor_tensor(C.wo_bc[:, :], wbc[:, 0, :], wbc[:, 1, :], ALU.add))
            L(V.tensor_tensor(dcol[:, :], wcols[:, 0:1], wcols[:, 1:2], ALU.subtract))
            dve.sem_inc(dcol_ready, 1)
            L(V.tensor_scalar(head_i[:, :], pidx_i[:, :], 4, None, ALU.logical_shift_right))
            L(V.tensor_copy(head_f[:, :], head_i[:, :]))
            L(V.tensor_scalar(C.headw[:, :], C.iota[:, 0:HEADS], head_f[:, :], float(HC) ** -0.5, ALU.is_equal, ALU.mult))
            L(V.tensor_copy(C.ext[:, :, 1], w_sb[:, :]))
            L(V.tensor_copy(C.ext[:, :, 2], dst_i[:, :]))
            dve.wait_ge(pe_made, 3)
            L(V.tensor_copy(C.wsk[:, D:D + 1], pu[:, 0:1]))
            L(V.tensor_copy(brow[:, 256 + D:257 + D], pu[0:1, 1:2]))
            L(V.memset(brow[:, 385:388], 0.0))
            for n in range(3):
                L(V.tensor_copy(bsplit[:, n, :], brow[:, :]))
                L(V.tensor_tensor(brow[:, :], brow[:, :], bsplit[:, n, :], ALU.subtract))
            dve.sem_inc(split_ready, 1)

        @block.tensor
        def _(pe):
            pe.wait_ge(block_oh, 1)
            for g in range(NG):
                pe.wait_ge(oh_made, g + 1)
                for j in range(GRP):
                    e = g * GRP + j
                    mm = nc.tensor.matmul(pcnt[:, :], oh_t[:, j, :], oh_b[:, e, :], start=(e == 0), stop=(e == EB - 1))
                mm.then_inc(oh_used, 1)
            pe.wait_ge(rounds_ready, 1)
            nc.tensor.matmul(ppre[:, :], upper[:, :], rt[:, :], start=True, stop=True).then_inc(pe_made, 1)
            pe.wait_ge(sel_ready, 1)
            nc.tensor.matmul(psel[:, :], quant[:, :], sel[:, :], start=True, stop=True)
            nc.tensor.matmul(pst[:, :], bc[:, 0, :], sel[:, :], start=True, stop=True)
            nc.tensor.matmul(pta[:, :], bc[:, 1, :], sel[:, :], start=True, stop=True)
            nc.tensor.matmul(psum1[:, :], onesf[0:TILES, 0:1], rt[:, :], start=True, stop=True).then_inc(pe_made, 1)
            pe.wait_ge(dcol_ready, 1)
            nc.tensor.matmul(pu[:, 0:1], wskT[:, :], dcol[:, :], start=True, stop=True)
            nc.tensor.matmul(pu[0:1, 1:2], bskc[:, :], dcol[:, :], start=True, stop=True).then_inc(pe_made, 1)


KINDS = {
    "sage1": dict(F=128, W=131, AW=130, tiles=(128,)),
    "sage2": dict(F=128, W=128, AW=128, tiles=(128, 128)),
    "attn": dict(F=0, W=136, AW=136, tiles=(128,)),
    "gcn1": dict(F=128, W=128, AW=128, tiles=(128,)),
    "gcn2": dict(F=256, W=256, AW=256, tiles=(256,)),
    "gcn3": dict(F=128, W=128, AW=128, tiles=(128, 128)),
    "pool": dict(F=128, W=128, AW=128, tiles=(128,)),
}


def conv_phase(nc, C, kind, gather_from, msgs, node_from, result):
    cfg = KINDS[kind]
    F, W, AW, widths = cfg["F"], cfg["W"], cfg["AW"], cfg["tiles"]
    HX = widths[0] // P
    gcn = kind.startswith("gcn")
    norm = kind in ("sage2", "gcn3", "pool")
    dense = kind not in ("gcn3", "attn")
    node_t = kind in ("sage1", "sage2", "attn")
    frees_psum = kind in ("sage1", "gcn1", "gcn2")
    OW = {"gcn1": HID, "attn": P}.get(kind, D)
    LA = {"sage1": 4, "sage2": 2, "attn": 4, "pool": 2}.get(kind, 3)
    LP = {"attn": 4, "sage2": 7, "pool": 7, "gcn3": 9}.get(kind, 0)
    ctx = ExitStack()
    with ctx:
        def sb(name, shape, dt=F32):
            return ctx.enter_context(nc.sbuf_tensor(f"{kind}_{name}", shape, dt))

        def ps(name, shape):
            return ctx.enter_context(nc.psum_tensor(f"{kind}_{name}", shape, F32))

        def sem(name):
            C.sems.append(ctx.enter_context(nc.semaphore(f"{kind}_{name}")))
            return C.sems[-1]

        gbuf = sb("gbuf", [P, 2, GB, W if F else 1])
        idx = sb("idx", [P, 2, GB], I32)
        win = sb("win", [P, U, NB, W])
        tile0 = sb("tile0", [P, U, NB, widths[0]])
        tile1 = sb("tile1", [P, U, NB, D]) if len(widths) > 1 else None
        onehot = sb("onehot", [P, U, NB, P])
        acc = sb("acc", [P, NB, AW])
        feat = sb("feat", [P, U, NB, HX * P])
        featT = sb("featT", [P, HX, NB, P])
        nodeT = sb("nodeT", [P, U, NB, P])
        y = sb("y", [P, U, NB, D])
        outb = sb("outb", [P, U, NB, OW])
        h2 = sb("h2", [P, NB, HID if kind == "gcn2" else 1])
        h2T = sb("h2T", [P, 2, NB, P if kind == "gcn2" else 1])
        small = sb("small", [P, U, 8, NB])
        stats = sb("stats", [P, U, NB, 6])
        mv = sb("mv", [P, U, NB, 3])
        rden = sb("rden", [P, NB, HEADS])
        escr = sb("escr", [P, NB, D])
        sink = sb("sink", [1, 1])
        prod = sb("prod", [P, U, NB, D]) if kind == "attn" else None
        xd = sb("xd", [P, U, NB, D]) if kind == "attn" else None
        hrow = sb("hrow", [P, U, NB, D]) if kind == "attn" else None
        AP = P if AW <= P else 2 * P
        pagg = ps("pagg", [P, NB, AP])
        pT = ps("pT", [P, HX, NB, P])
        pN = ps("pN", [P, NB, P]) if node_t else None
        OP = {"gcn1": 256, "gcn2": 256, "attn": 256}.get(kind, P)
        pout = ps("pout", [P, NB, OP]) if kind != "gcn3" else None
        pz = ps("pz", [P, NB, P]) if kind == "gcn2" else None

        flushed = sem("flushed")
        paced, stores_paced = sem("paced"), sem("stores_paced")
        idx_ready = sem("idx_ready")
        gathered = C.gathered.get(kind)
        rows_in = C.rows_in.get(kind)
        win_in = [sem(f"win_in{k}") for k in range(U)]
        tile_in = [sem(f"tile_in{k}") for k in range(U)]
        out_in = [sem(f"out_in{k}") for k in range(U)]
        gated = [sem(f"gated{c}") for c in range(4)]
        rel_made = sem("rel_made")
        onehot_ready = sem("onehot_ready")
        agg_done = sem("agg_done")
        acc_chain = sem("acc_chain")
        post_chain = sem("post_chain")
        featT_ps, featT_ready = sem("featT_ps"), sem("featT_ready")
        nodeT_ps, nodeT_ready = sem("nodeT_ps"), sem("nodeT_ready")
        out_ps = sem("out_ps")
        out_ready = sem("out_ready")
        act_small = sem("act_small")
        exp_done = sem("exp_done")
        acc_zeroed = sem("acc_zeroed")
        helper = sem("helper")
        h2_ready, h2T_ps, h2T_ready, z_ps = sem("h2_ready"), sem("h2T_ps"), sem("h2T_ready"), sem("z_ps")
        stats_made = sem("stats_made")
        block = ctx.enter_context(nc.Block())

        def trips(eng):
            return eng.value_load(C.trips[0:1, 0:1], min_val=TILES // U, max_val=(STEPS - 4) // U)

        def step_loop(eng, body, after=None):
            n = trips(eng)
            for i in range(2):
                for k in range(U):
                    body(i, k)
            with eng.Fori(2, n) as i:
                for k in range(U):
                    body(i, k)
            if after is not None:
                after(n, eng.value_load(C.trips[0:1, 1:2], min_val=1, max_val=(STEPS - 4) // U - 1))

        def ahead(i, k, d):
            return i + (k + d) // U, (k + d) % U

        def tau_of(eng, s):
            return eng.value_load(C.meta[0:1, ds(META * s + 7, 1)], min_val=0, max_val=TILES - 1)

        def load_row(eng, s, c, n, most):
            return nc.values_load_multi_w_load_instructions(
                C.meta[0:1, ds(META * s + c, n)], engines=(eng.engine,), min_val=0, max_val=most)[1]

        @block.sync
        def _(sp):
            def windows(i, k):
                s = U * i + k
                w = load_row(sp, s, 0, NB, EDGES)
                node, even, odd = load_row(sp, s, 4, 3, (TILES - 1) * TILE)
                if F:
                    sp.wait_ge(rows_in[0], even)
                    sp.wait_ge(rows_in[1], odd)
                for b in range(NB):
                    sp.dma_start(win[:, k, b, :], msgs[ds(w[b], P), :]).then_inc(win_in[k], 16)
                return node

            def tiles(node, k):
                sp.dma_start(tile0[:, k, :, :], rows_at(node_from[0], node)).then_inc(tile_in[k], 16)
                if tile1 is not None:
                    sp.dma_start(tile1[:, k, :, :], rows_at(node_from[1], node)).then_inc(tile_in[k], 16)

            for k in range(U):
                tiles(windows(0, k), k)

            def body(i, k):
                s = U * i + k
                sp.wait_ge(agg_done, s + 1)
                node = windows(i + 1, k)
                if kind == "sage1":
                    sp.wait_ge(nodeT_ps, s + 1)
                elif kind in ("gcn1", "gcn2"):
                    sp.wait_ge(acc_chain, LA * s + 2)
                elif kind == "attn":
                    sp.wait_ge(helper, 2 * (s + 1))
                    sp.wait_ge(nodeT_ps, s + 1)
                else:
                    sp.wait_ge(post_chain, LP * s + (4 if kind == "gcn3" else 1))
                    if kind == "sage2":
                        sp.wait_ge(nodeT_ps, s + 1)
                tiles(node, k)

            def after(n, m):
                for k in range(U):
                    sp.wait_ge(win_in[k], 16 * NB * (n + 1))
                    sp.sem_inc(paced, 1)
                    sp.wait_ge(tile_in[k], 16 * len(widths) * (n + 1))
                    sp.sem_inc(paced, 1)
                sp.dma_start(sink[:, :], C.bounce[0:1, 0:1]).then_inc(flushed, 16)
                sp.wait_ge(flushed, 16)

            step_loop(sp, body, after)

        @block.gpsimd
        def _(pool):
            if kind == "attn":
                def body(i, k):
                    s = U * i + k
                    if not (isinstance(i, int) and i == 0):
                        pool.wait_ge(post_chain, LP * (s - 2))
                    pool.wait_ge(acc_chain, LA * (s + 1))
                    nc.gpsimd.tensor_tensor(prod[:, k, :, :], feat[:, k, :, :],
                                            C.wo_bc[:, :].unsqueeze(1).to_broadcast([P, NB, D]), ALU.mult)\
                        .then_inc(helper, 1)
                    pool.wait_ge(tile_in[k], 16 * (i + 1))
                    nc.gpsimd.tensor_tensor(y[:, k, :, :], feat[:, k, :, :], tile0[:, k, :, :], ALU.add)\
                        .then_inc(helper, 1)
                step_loop(pool, body)
                return

            def gate(i, c):
                if not (isinstance(i, int) and i == 0):
                    pool.wait_ge(gated[c], i)
                g = C.gate_out[:, c:c + 1]
                nc.gpsimd.tensor_tensor(g, C.gate[:, :], C.gate[:, :], ALU.mult).then_inc(gated[c], 1)

            def store_rows(i, q):
                pool.wait_ge(gathered[q], 16 * GB * (i + 1))
                gate(i, q)
                rows = msgs[ds((2 * i + q) * GB * P, GB * P), :].rearrange("(b p) f -> p b f", p=P)
                pool.dma_start(rows, gbuf[:, q, :, :]).then_inc(rows_in[q], 16)

            def batch(i, q):
                first = isinstance(i, int)
                k = 2 * i + q
                if not first:
                    pool.wait_ge(rows_in[q], 16 * i)
                if kind == "sage1":
                    nc.gpsimd.tensor_copy(gbuf[:, q, :, 128:131], C.ext[:, ds(k * GB, GB), :])
                nc.gpsimd.tensor_copy(idx[:, q, :], C.src_sb[:, ds(k * GB, GB)]).then_inc(idx_ready, 1)
                pool.wait_ge(idx_ready, k + 1)
                gate(i, 2 + q)
                for j in range(GB):
                    pool.indirect_dma_start(
                        out=gbuf[:, q, j, 0:F], out_offset=None, in_=gather_from,
                        in_offset=bass.IndirectOffsetOnAxis(ap=idx[:, q, j:j + 1], axis=0)).then_inc(gathered[q], 16)
                if q == 1:
                    store_rows(i, 0)
                elif not first:
                    store_rows(i - 1, 1)

            batch(0, 0)
            batch(0, 1)
            with pool.Fori(1, BATCHES // 2) as i:
                batch(i, 0)
                batch(i, 1)
            store_rows(BATCHES // 2 - 1, 1)
            pool.wait_ge(rows_in[0], 16 * (BATCHES // 2))
            pool.wait_ge(rows_in[1], 16 * (BATCHES // 2))

        @block.vector
        def _(dve):
            V = nc.vector
            a, p = Chain(dve, acc_chain, LA), Chain(dve, post_chain, LP)

            def make_onehot(i, k):
                t = U * i + k
                if not (isinstance(i, int) and i == 0):
                    dve.wait_ge(agg_done, t - 2)
                tab = C.dst_tab[:, ds(NB * t, NB)]
                if kind == "sage1":
                    dve.wait_ge(win_in[k], 16 * NB * (i + 1))
                    rel = small[:, k, 0, :]
                    V.tensor_scalar(rel, win[:, k, :, 130], C.base[:, ds(t, 1)], None, ALU.subtract)\
                        .then_inc(rel_made, 1)
                    V.tensor_copy(C.w_tab[:, ds(NB * t, NB)], win[:, k, :, 129])
                    dve.wait_ge(rel_made, t + 1)
                    V.tensor_copy(tab, rel)
                    tab = rel
                iota = C.iota[:, :].rearrange("p (b n) -> p b n", b=NB)
                oh = onehot[:, k, :, :]
                ins = V.tensor_tensor(oh, iota, tab.unsqueeze(2).to_broadcast([P, NB, P]), ALU.is_equal)
                if gcn:
                    ins.then_inc(rel_made, 1)
                    dve.wait_ge(rel_made, t + 1)
                    wt = C.w_tab[:, ds(NB * t, NB)]
                    ins = V.tensor_tensor(oh, oh, wt.unsqueeze(2).to_broadcast([P, NB, P]), ALU.mult)
                ins.then_inc(onehot_ready, 1)

            def accumulate(i, k):
                s = U * i + k
                a.begin(s)
                tau = tau_of(dve, s)
                if not (isinstance(i, int) and s == 0) and not gcn:
                    dve.wait_ge(acc_chain, LA * s)
                dve.wait_ge(agg_done, s + 1)
                a.link(V.scalar_tensor_tensor(acc[:, :, :], acc[:, :, :], C.keep[:, ds(s, 1)], pagg[:, :, 0:AW],
                                              ALU.mult, ALU.add))
                f = feat[:, k, :, :]

                def over_rows(v, w):
                    return v.unsqueeze(2).to_broadcast([P, NB, w])

                if kind == "sage1":
                    V.tensor_copy(C.deg[:, ds(NB * tau, NB)], acc[:, :, 129])
                    a.link(V.tensor_scalar(small[:, k, 1, :], acc[:, :, 128], 1.0, None, ALU.max))
                    a.link(V.reciprocal(small[:, k, 2, :], small[:, k, 1, :]))
                    V.tensor_copy(C.inv_cnt[:, ds(NB * tau, NB)], small[:, k, 2, :])
                    a.mark(V.tensor_tensor(f, acc[:, :, 0:D], over_rows(small[:, k, 2, :], D), ALU.mult))
                elif kind in ("sage2", "pool"):
                    a.mark(V.tensor_tensor(f, acc[:, :, :], over_rows(C.inv_cnt[:, ds(NB * tau, NB)], D), ALU.mult))
                elif kind == "attn":
                    a.link(V.tensor_scalar(rden[:, :, :], acc[:, :, D:D + HEADS], 1e-16, None, ALU.add))
                    a.link(V.reciprocal(rden[:, :, :], rden[:, :, :]))
                    a.mark(V.tensor_tensor(f.rearrange("p b (h c) -> p b h c", c=HC),
                                           acc[:, :, 0:D].rearrange("p b (h c) -> p b h c", c=HC),
                                           rden[:, :, :].unsqueeze(3).to_broadcast([P, NB, HEADS, HC]), ALU.mult))
                else:
                    dve.wait_ge(tile_in[k], 16 * len(widths) * (i + 1))
                    a.link(V.tensor_tensor(f, acc[:, :, :], tile0[:, k, :, :], ALU.add))
                    a.link(V.tensor_tensor(f, f, over_rows(C.dinv[:, ds(NB * tau, NB)], HX * P), ALU.mult))

            def layernorm_stats(k):
                for b in range(NB):
                    ins = V.bn_stats(stats[:, k, b, :], y[:, k, b, :])
                p.link(ins)
                row_variance(V, p, stats[:, k, :, :], mv[:, k, :, :], small[:, k, 3, :])

            def layernorm_scale(s, k, nth):
                dve.wait_ge(act_small, nth)
                p.link(V.reciprocal(small[:, k, 5, :], small[:, k, 4, :])) if kind != "gcn3" else None
                rs = small[:, k, 5, :]
                p.mark(V.scalar_tensor_tensor(small[:, k, 6, :], mv[:, k, :, 0], -0.5, rs, ALU.mult, ALU.mult))

            def post(i, k):
                s = U * i + k
                p.begin(s)
                if kind in ("sage2", "pool"):
                    dve.wait_ge(out_ps, s + 1)
                    if kind == "sage2":
                        dve.wait_ge(tile_in[k], 32 * (i + 1))
                        p.link(V.tensor_tensor(y[:, k, :, :], pout[:, :, :], tile1[:, k, :, :], ALU.add))
                    else:
                        dve.wait_ge(tile_in[k], 16 * (i + 1))
                        p.link(V.scalar_tensor_tensor(y[:, k, :, :], pout[:, :, :], 0.0, tile0[:, k, :, :],
                                                      ALU.max, ALU.add))
                    layernorm_stats(k)
                elif kind == "gcn3":
                    u = feat[:, k, :, :]
                    p.link(V.tensor_tensor(u, u, C.bl_bc[:, :].unsqueeze(1).to_broadcast([P, NB, D]), ALU.add))
                    p.link(V.tensor_reduce(small[:, k, 0, :], u, AX.X, ALU.max))
                    p.mark(V.tensor_scalar(small[:, k, 1, :], small[:, k, 0, :], -1.0, None, ALU.mult))
                elif kind == "attn":
                    dve.wait_ge(helper, 2 * s + 1)
                    p.link(V.tensor_reduce(small[:, k, 0, :], prod[:, k, :, :], AX.X, ALU.add))
                    dve.wait_ge(out_ps, s + 1)
                    p.mark(V.tensor_tensor(small[:, k, 1, :], small[:, k, 0, :], pout[:, :, D], ALU.add))
                    p.mark(V.tensor_tensor(xd[:, k, :, :], pout[:, :, 0:D], feat[:, k, :, :], ALU.subtract))

            def finish_post(i, k):
                s = U * i + k
                if kind in ("sage2", "pool"):
                    p.resume(s, 5)
                    layernorm_scale(s, k, s + 1)
                elif kind == "gcn3":
                    p.resume(s, 3)
                    u = feat[:, k, :, :]
                    dve.wait_ge(act_small, 2 * s + 1)
                    V.scalar_tensor_tensor(small[:, k, 7, :], small[:, k, 2, :], -1.0, small[:, k, 1, :],
                                           ALU.mult, ALU.add).then_inc(stats_made, 1)
                    dve.wait_ge(stats_made, s + 1)
                    for b in range(NB):
                        ins = V.scalar_tensor_tensor(y[:, k, b, :], u[:, b, :], small[:, k, 7, b:b + 1],
                                                     tile1[:, k, b, :], ALU.add, ALU.add)
                    p.link(ins)
                    layernorm_stats(k)
                    layernorm_scale(s, k, 2 * s + 2)
                else:
                    p.resume(s, 3)
                    dve.wait_ge(post_chain, LP * s + 3)
                    dve.wait_ge(act_small, s + 1)
                    dve.wait_ge(helper, 2 * s + 2)
                    for b in range(NB):
                        ins = V.scalar_tensor_tensor(hrow[:, k, b, :], xd[:, k, b, :], small[:, k, 2, b:b + 1],
                                                     y[:, k, b, :], ALU.mult, ALU.add)
                    p.mark(ins)

            def graph_stats(i, k):
                s = U * i + k
                tau = tau_of(dve, s)
                if not (isinstance(i, int) and s == 0):
                    dve.wait_ge(stats_made, s)
                dve.wait_ge(out_ready, s + 1)
                V.bn_stats(C.gstats[:, ds(6 * tau, 6)], outb[:, k, :, :].rearrange("p b n -> p (b n)"))\
                    .then_inc(stats_made, 1)

            V.memset(acc[:, :, :], 0.0).then_inc(acc_zeroed, 1)
            dve.wait_ge(acc_zeroed, 1)
            make_onehot(0, 0)
            make_onehot(0, 1)
            accumulate(0, 0)

            def body(i, k):
                make_onehot(*ahead(i, k, 2))
                accumulate(*ahead(i, k, 1))
                if norm and not (isinstance(i, int) and i == k == 0):
                    finish_post(*ahead(i - 1, k, U - 1))
                if LP:
                    post(i, k)
                if kind == "attn":
                    finish_post(i, k)
                if kind == "attn" and not (isinstance(i, int) and i == k == 0):
                    graph_stats(*ahead(i - 1, k, U - 1))

            last = graph_stats if kind == "attn" else finish_post if norm else None
            step_loop(dve, body, last and (lambda n, m: last(m, U - 1)))

        @block.tensor
        def _(pe):
            T = nc.tensor

            def bias(out, name, at=0, n=None, start=True):
                o, w = BROW[name]
                w = n or w
                T.matmul(out, C.ones3[:, :], C.bias3[:, o + at:o + at + w], start=start, stop=False)

            def sums(i, k):
                t = U * i + k
                pe.wait_ge(onehot_ready, t + 1)
                pe.wait_ge(win_in[k], 16 * NB * (i + 1))
                if not (isinstance(i, int) and t == 0):
                    pe.wait_ge(acc_chain, LA * (t - 1) + 1)
                for b in range(NB):
                    mm = T.matmul(pagg[:, b, 0:AW], onehot[:, k, b, :], win[:, k, b, 0:AW], start=True, stop=True)
                mm.then_inc(agg_done, 1)

            def transpose_sums(i, k):
                s = U * i + k
                if kind == "attn":
                    pe.wait_ge(post_chain, LP * (s + 1))
                else:
                    pe.wait_ge(acc_chain, LA * (s + 1))
                if not (isinstance(i, int) and s == 0):
                    pe.wait_ge(out_ready if kind == "attn" else featT_ready, s)
                    if kind == "gcn2" and not (isinstance(i, int) and s == 1):
                        pe.wait_ge(h2T_ready, s - 1)
                for c in range(HX):
                    for b in range(NB):
                        rows = hrow if kind == "attn" else feat
                        mm = T.transpose(pT[:, c, b, :], rows[:, k, b, c * P:(c + 1) * P], C.ident[:, :])
                mm.then_inc(featT_ps, 1)

            def transpose_nodes(i, k):
                t = U * i + k
                pe.wait_ge(tile_in[k], 16 * len(widths) * (i + 1))
                if not (isinstance(i, int) and t == 0):
                    pe.wait_ge(nodeT_ready, t)
                for b in range(NB):
                    mm = T.transpose(pN[:, b, :], tile0[:, k, b, :], C.ident[:, :])
                mm.then_inc(nodeT_ps, 1)

            def products(i, k):
                s = U * i + k
                if kind != "attn":
                    pe.wait_ge(featT_ready, s + 1)
                if node_t:
                    pe.wait_ge(nodeT_ready, s + 1)
                if not (isinstance(i, int) and s == 0):
                    if kind in ("sage1", "gcn1"):
                        pe.wait_ge(out_ready, s)
                    elif kind == "gcn2":
                        pe.wait_ge(h2_ready, s)
                    elif kind == "attn":
                        pe.wait_ge(post_chain, LP * (s - 1) + 3)
                    else:
                        pe.wait_ge(post_chain, LP * (s - 1) + 1)
                for b in range(NB):
                    if kind in ("sage1", "sage2"):
                        wl, wr = (C.w1l, C.w1r) if kind == "sage1" else (C.w2l, C.w2r)
                        bias(pout[:, b, :], "b1l" if kind == "sage1" else "b2l")
                        T.matmul(pout[:, b, :], nodeT[:, k, b, :], wr[:, :], start=False, stop=False)
                        mm = T.matmul(pout[:, b, :], featT[:, 0, b, :], wl[:, :], start=False, stop=True)
                    elif kind == "pool":
                        bias(pout[:, b, :], "pool")
                        mm = T.matmul(pout[:, b, :], featT[:, 0, b, :], C.wp[:, :], start=False, stop=True)
                    elif kind == "attn":
                        bias(pout[:, b, 0:D + 1], "skip")
                        mm = T.matmul(pout[:, b, 0:D + 1], nodeT[:, k, b, :], C.wsk[:, :], start=False, stop=True)
                    elif kind == "gcn1":
                        bias(pout[:, b, :], "gcn0")
                        mm = T.matmul(pout[:, b, :], featT[:, 0, b, :], C.wg0[:, :], start=False, stop=True)
                    else:
                        bias(pout[:, b, :], "gcn1")
                        T.matmul(pout[:, b, :], featT[:, 0, b, :], C.wg1[:, 0, :], start=False, stop=False)
                        mm = T.matmul(pout[:, b, :], featT[:, 1, b, :], C.wg1[:, 1, :], start=False, stop=True)
                mm.then_inc(out_ps, 1)

            def transpose_h2(i, k, last=False):
                s = U * i + k
                pe.wait_ge(h2_ready, s + 1)
                if not last:
                    pe.wait_ge(featT_ready, s + 2)
                for c in range(2):
                    for b in range(NB):
                        mm = T.transpose(pT[:, c, b, :], h2[:, b, c * P:(c + 1) * P], C.ident[:, :])
                mm.then_inc(h2T_ps, 1)

            def last_product(i, k):
                s = U * i + k
                pe.wait_ge(h2T_ready, s + 1)
                if not (isinstance(i, int) and s == 0):
                    pe.wait_ge(out_ready, s)
                for b in range(NB):
                    for c in range(2):
                        mm = T.matmul(pz[:, b, :], h2T[:, c, b, :], C.wgl[:, c, :], start=(c == 0), stop=(c == 1))
                mm.then_inc(z_ps, 1)

            sums(0, 0)
            if node_t:
                transpose_nodes(0, 0)

            def body(i, k):
                if kind == "attn":
                    products(i, k)
                elif dense:
                    transpose_sums(i, k)
                sums(*ahead(i, k, 1))
                if node_t:
                    transpose_nodes(*ahead(i, k, 1))
                start = isinstance(i, int) and i == k == 0
                if kind == "gcn2" and not start:
                    transpose_h2(*ahead(i - 1, k, U - 1))
                if dense:
                    products(i, k)
                if kind == "gcn2" and not start:
                    last_product(*ahead(i - 1, k, U - 1))
                if kind == "attn" and not start:
                    transpose_sums(*ahead(i - 1, k, U - 1))

            def after(n, m):
                if kind == "gcn2":
                    transpose_h2(m, U - 1, last=True)
                    last_product(m, U - 1)
                if kind == "attn":
                    transpose_sums(m, U - 1)

            step_loop(pe, body, after if kind in ("gcn2", "attn") else None)

        @block.scalar
        def _(act):
            S = nc.scalar

            def read_sumsT(i, k):
                s = U * i + k
                act.wait_ge(featT_ps, s + 1)
                S.activation(featT[:, :, :, :], pT[:, :, :, :], ACT.Copy).then_inc(featT_ready, 1)

            def read_nodesT(i, k):
                t = U * i + k
                act.wait_ge(nodeT_ps, t + 1)
                S.activation(nodeT[:, k, :, :], pN[:, :, :], ACT.Copy).then_inc(nodeT_ready, 1)

            def slot_free(i, k):
                if not isinstance(i, int) or i > 0:
                    act.wait_ge(out_in[k], 16 * i)

            def final(i, k):
                s = U * i + k
                slot_free(i, k)
                if kind == "sage1":
                    act.wait_ge(out_ps, s + 1)
                    S.activation(outb[:, k, :, :], pout[:, :, :], ACT.Relu).then_inc(out_ready, 1)
                elif kind == "gcn1":
                    tau = tau_of(act, s)
                    act.wait_ge(out_ps, s + 1)
                    for b in range(NB):
                        ins = S.activation(outb[:, k, b, :], pout[:, b, :], ACT.Relu,
                                           scale=C.dinv[:, ds(NB * tau + b, 1)])
                    ins.then_inc(out_ready, 1)
                elif norm:
                    act.wait_ge(post_chain, LP * (s + 1))
                    for b in range(NB):
                        ins = S.activation(outb[:, k, b, :], y[:, k, b, :], ACT.Identity,
                                           bias=small[:, k, 6, b:b + 1], scale=small[:, k, 5, b:b + 1])
                    ins.then_inc(out_ready, 1)

            def read_h2(i, k):
                s = U * i + k
                tau = tau_of(act, s)
                act.wait_ge(out_ps, s + 1)
                for b in range(NB):
                    ins = S.activation(h2[:, b, :], pout[:, b, :], ACT.Relu, scale=C.dinv[:, ds(NB * tau + b, 1)])
                ins.then_inc(h2_ready, 1)

            def read_h2T(i, k):
                act.wait_ge(h2T_ps, U * i + k + 1)
                S.activation(h2T[:, :, :, :], pT[:, :, :, :], ACT.Copy).then_inc(h2T_ready, 1)

            def read_z(i, k):
                slot_free(i, k)
                act.wait_ge(z_ps, U * i + k + 1)
                S.activation(outb[:, k, :, :], pz[:, :, :], ACT.Copy).then_inc(out_ready, 1)

            def deviation(i, k):
                s = U * i + k
                if kind == "gcn3":
                    act.wait_ge(post_chain, LP * s + 3)
                    for b in range(NB):
                        ins = S.activation(escr[:, b, :], feat[:, k, b, :], ACT.Exp, bias=small[:, k, 1, b:b + 1],
                                           accum_out=small[:, k, 3, b:b + 1])
                        ins.then_inc(exp_done, 1)
                    act.wait_ge(exp_done, 4 * s + 4)
                    S.activation(small[:, k, 2, :], small[:, k, 3, :], ACT.Ln).then_inc(act_small, 1)
                    act.wait_ge(post_chain, LP * s + 8)
                    S.activation(small[:, k, 4, :], small[:, k, 3, :], ACT.Ln).then_inc(featT_ready, 1)
                    act.wait_ge(featT_ready, s + 1)
                    S.activation(small[:, k, 5, :], small[:, k, 4, :], ACT.Exp, scale=-0.5).then_inc(act_small, 1)
                else:
                    act.wait_ge(post_chain, LP * s + 5)
                    S.activation(small[:, k, 4, :], small[:, k, 3, :], ACT.Sqrt).then_inc(act_small, 1)

            def beta(i, k):
                s = U * i + k
                act.wait_ge(post_chain, LP * s + 2)
                S.activation(small[:, k, 2, :], small[:, k, 1, :], ACT.Sigmoid).then_inc(act_small, 1)

            def read_hT(i, k):
                s = U * i + k
                act.wait_ge(featT_ps, s + 1)
                slot_free(i, k)
                if not isinstance(i, int) or i > 0:
                    act.wait_ge(stats_made, s - 2)
                S.activation(outb[:, k, :, :], pT[:, 0, :, :], ACT.Copy).then_inc(out_ready, 1)

            def store(i, k):
                s = U * i + k
                node = load_row(act, s, 4, 1, (TILES - 1) * TILE)[0]
                pi, pk = ahead(i - 1, k, U - 1)
                if not (isinstance(i, int) and i == k == 0):
                    act.wait_ge(out_in[pk], 16 * (pi + 1))
                    act.sem_inc(stores_paced, 1)
                act.wait_ge(out_ready, s + 1)
                if kind == "attn":
                    act.sem_inc(stores_paced, 1)
                    act.dma_start(result[:, ds(node, TILE)], outb[:, k, :, :].rearrange("p b n -> p (b n)"))\
                        .then_inc(out_in[k], 16)
                else:
                    act.dma_start(rows_at(result, node), outb[:, k, :, :]).then_inc(out_in[k], 16)

            if node_t:
                read_nodesT(0, 0)

            def body(i, k):
                if dense:
                    read_sumsT(i, k)
                if node_t:
                    read_nodesT(*ahead(i, k, 1))
                stored = not (isinstance(i, int) and i == 0 and k < 2)
                if stored and not frees_psum:
                    store(*ahead(i - 1, k, U - 2))
                start = isinstance(i, int) and i == k == 0
                before = ahead(i - 1, k, U - 1)
                if kind == "gcn2":
                    if not start:
                        read_h2T(*before)
                    read_h2(i, k)
                    if not start:
                        read_z(*before)
                    if stored:
                        store(*ahead(i - 1, k, U - 2))
                    return
                if kind == "attn":
                    beta(i, k)
                if not start:
                    finish(*before)
                if stored and frees_psum:
                    store(*ahead(i - 1, k, U - 2))

            def finish(i, k):
                if kind == "attn":
                    read_hT(i, k)
                    return
                if kind == "gcn2":
                    read_h2T(i, k)
                    read_z(i, k)
                    return
                if norm:
                    deviation(i, k)
                final(i, k)

            def after(n, m):
                finish(m, U - 1)
                store(m, U - 2)
                store(m, U - 1)
                for k in range(U):
                    act.wait_ge(out_in[k], 16 * n)
                    act.sem_inc(stores_paced, 1)

            step_loop(act, body, after)


def batches(eng, body):
    for q in range(2):
        body(0, q, True, q == 0)
    with eng.Fori(1, ETILES // 2) as i:
        for q in range(2):
            body(i, q, False, False)
    body(ETILES // 2, 0, False, False)


def edge_scores_phase(nc, C, A):
    B, W = EBATCH, ETILE
    ctx = ExitStack()
    with ctx:
        def sb(name, shape, dt=F32):
            return ctx.enter_context(nc.sbuf_tensor("es_" + name, shape, dt))

        def ps(name, shape):
            return ctx.enter_context(nc.psum_tensor("es_" + name, shape, F32))

        def sem(name):
            C.sems.append(ctx.enter_context(nc.semaphore("es_" + name)))
            return C.sems[-1]

        idx = sb("idx", [P, 2, 2, B], I32)
        gx = sb("gx", [P, 2, 2, B, D])
        gT = sb("gT", [P, 2, B, P])
        ea = sb("ea", [11, 2, W])
        dT = sb("dT", [HEADS, 2, W + 2], I32)
        q_sb = sb("q_sb", [P, W])
        prod = sb("prod", [P, W])
        v_sb = sb("v_sb", [P, 2, B, D])
        al = sb("al", [HEADS, 2, W])
        cut = sb("cut", [HEADS, 2, W])
        fm = sb("fm", [HEADS, 2, W])
        dg = sb("dg", [P, 2, NB * TILES])
        pX = [ps("pX0", [P, B, P]), ps("pX1", [P, B, P])]
        pq, pk, pv, pa = ps("pq", [P, W]), ps("pk", [P, W]), ps("pv", [P, B, D]), ps("pa", [HEADS, W])

        gated = [sem("gated0"), sem("gated1")]
        ones_made, idx_ready = sem("ones_made"), sem("idx_ready")
        gathered = C.gathered["scores"]
        rows_in = [sem("rows_in0"), sem("rows_in1")]
        stored = [sem("stored0"), sem("stored1")]
        x_ps, xT_ready = sem("x_ps"), sem("xT_ready")
        kq_ps, v_ps = sem("kq_ps"), sem("v_ps")
        q_ready, prod_ready = sem("q_ready"), sem("prod_ready")
        a_ps, a_ready = sem("a_ps"), sem("a_ready")
        v_ready = sem("v_ready")
        cut_made, fm_ready = sem("cut_made"), sem("fm_ready")
        deg_chain, deg_root = sem("deg_chain"), sem("deg_root")
        block = ctx.enter_context(nc.Block())


        @block.gpsimd
        def _(pool):
            nc.gpsimd.memset(ea[:, :, :], 1.0).then_inc(ones_made, 1)

            def body(i, q, new, first):
                n = 2 * i + q
                if not new:
                    pool.wait_ge(x_ps, 2 * (n - 1))
                nc.gpsimd.tensor_copy(idx[:, q, 0, :], C.src_sb[:, ds(n * B, B)]).then_inc(idx_ready, 1)
                nc.gpsimd.tensor_copy(idx[:, q, 1, :], C.dst_sb[:, ds(n * B, B)]).then_inc(idx_ready, 1)
                pool.wait_ge(idx_ready, 2 * n + 2)
                if not new:
                    pool.wait_ge(gated[q], i)
                nc.gpsimd.tensor_tensor(C.gate_out[:, q:q + 1], C.gate[:, :], C.gate[:, :], ALU.mult)\
                    .then_inc(gated[q], 1)
                for c in range(2):
                    for j in range(B):
                        pool.indirect_dma_start(
                            out=gx[:, q, c, j, :], out_offset=None, in_=C.x1[:, :],
                            in_offset=bass.IndirectOffsetOnAxis(ap=idx[:, q, c, j:j + 1], axis=0))\
                            .then_inc(gathered[q], 16)
            batches(pool, body)

        @block.sync
        def _(sp):
            sp.wait_ge(ones_made, 1)

            def body(i, q, new, first):
                n = 2 * i + q
                if not new:
                    sp.wait_ge(v_ps, n - 1)
                    sp.wait_ge(fm_ready, n - 1)
                sp.dma_start(ea[0:10, q, :], A.ea_rows[:, ds(n * W, W)]).then_inc(rows_in[q], 16)
                sp.dma_start(dT[:, q, :], A.dst_row[:, ds(n * W, W + 2)].partition_broadcast(HEADS)[:, 0, :])\
                    .then_inc(rows_in[q], 16)
            batches(sp, body)

        @block.tensor
        def _(pe):
            T = nc.tensor

            def body(i, q, new, first):
                n = 2 * i + q
                pe.wait_ge(gathered[q], 16 * 2 * B * (i + 1))
                for c in range(2):
                    if not first:
                        pe.wait_ge(xT_ready, 2 * n - 1 + c)
                    for j in range(B):
                        mm = T.transpose(pX[c][:, j, :], gx[:, q, c, j, :], C.ident[:, :])
                    mm.then_inc(x_ps, 1)
                pe.wait_ge(rows_in[q], 32 * (i + 1))
                pe.wait_ge(xT_ready, 2 * n + 2)
                if not first:
                    pe.wait_ge(prod_ready, n)
                T.matmul(pq[:, :], C.wq[:, :], gT[:, 1, :, :], start=True, stop=True)
                T.matmul(pk[:, :], C.wk[:, :], gT[:, 0, :, :], start=True, stop=False)
                T.matmul(pk[:, :], C.wek[:, :], ea[:, q, :], start=False, stop=True).then_inc(kq_ps, 1)
                if not first:
                    pe.wait_ge(v_ready, n)
                for j in range(B):
                    T.matmul(pv[:, j, :], gT[:, 0, j, :], C.wv[:, :], start=True, stop=False)
                    mm = T.matmul(pv[:, j, :], ea[:, q, j * P:(j + 1) * P], C.wev[:, :], start=False, stop=True)
                mm.then_inc(v_ps, 1)
                pe.wait_ge(prod_ready, n + 1)
                if not first:
                    pe.wait_ge(a_ready, n)
                T.matmul(pa[:, :], C.headw[:, :], prod[:, :], start=True, stop=True).then_inc(a_ps, 1)
            batches(pe, body)

        @block.scalar
        def _(act):
            S = nc.scalar
            act.wait_ge(deg_chain, 2)
            S.activation(dg[:, 1, :], dg[:, 0, :], ACT.Sqrt).then_inc(deg_root, 1)

            def body(i, q, new, first):
                n = 2 * i + q
                for c in range(2):
                    act.wait_ge(x_ps, 2 * n + 1 + c)
                    S.activation(gT[:, c, :, :], pX[c][:, :, :], ACT.Copy).then_inc(xT_ready, 1)
                act.wait_ge(kq_ps, n + 1)
                S.activation(q_sb[:, :], pq[:, :], ACT.Identity, bias=C.bq[:, :]).then_inc(q_ready, 1)
                act.wait_ge(v_ps, n + 1)
                if not new:
                    act.wait_ge(stored[q], 48 * i)
                S.activation(v_sb[:, q, :, :], pv[:, :, :], ACT.Copy).then_inc(v_ready, 1)
                act.wait_ge(a_ps, n + 1)
                S.activation(al[:, q, :], pa[:, :], ACT.Copy).then_inc(a_ready, 1)
                act.wait_ge(v_ready, n + 1)
                act.dma_start(C.v_e[ds(n * W, W), :].rearrange("(b p) f -> p b f", p=P), v_sb[:, q, :, :])\
                    .then_inc(stored[q], 16)
                act.wait_ge(a_ready, n + 1)
                act.dma_start(C.alphaT[:, ds(n * W, W)], al[:, q, :]).then_inc(stored[q], 16)
                act.wait_ge(fm_ready, n + 1)
                act.dma_start(C.fmaxT[:, ds(n * W, W)], fm[:, q, :]).then_inc(stored[q], 16)
            batches(act, body)
            act.wait_ge(stored[0], 48 * (ETILES // 2 + 1))
            act.wait_ge(stored[1], 48 * (ETILES // 2))

        @block.vector
        def _(dve):
            V = nc.vector
            V.tensor_scalar(C.dinv[:, :], C.deg[:, :], 1.0, 0.0, ALU.add, ALU.is_gt)
            V.tensor_scalar(dg[:, 0, :], C.deg[:, :], 1.0, 1e-30, ALU.add, ALU.max).then_inc(deg_chain, 2)
            dve.wait_ge(deg_root, 1)
            V.reciprocal(dg[:, 1, :], dg[:, 1, :]).then_inc(deg_chain, 1)
            dve.wait_ge(deg_chain, 3)
            V.tensor_tensor(C.dinv[:, :], C.dinv[:, :], dg[:, 1, :], ALU.mult)

            def body(i, q, new, first):
                n = 2 * i + q
                dve.wait_ge(rows_in[q], 32 * (i + 1))
                V.tensor_tensor(cut[:, q, :], dT[:, q, 1:W + 1], dT[:, q, 0:W], ALU.not_equal).then_inc(cut_made, 1)
                dve.wait_ge(cut_made, 2 * n + 1)
                V.tensor_scalar(cut[:, q, :], cut[:, q, :], -BIG, None, ALU.mult).then_inc(cut_made, 1)
                dve.wait_ge(q_ready, n + 1)
                V.tensor_tensor(prod[:, :], pk[:, :], q_sb[:, :], ALU.mult).then_inc(prod_ready, 1)
                dve.wait_ge(a_ready, n + 1)
                dve.wait_ge(cut_made, 2 * n + 2)
                if not first:
                    dve.wait_ge(fm_ready, n)
                if not new:
                    dve.wait_ge(stored[q], 48 * i)
                V.tensor_tensor_scan(fm[:, q, :], cut[:, q, :], al[:, q, :],
                                     -BIG if first else fm[:, 1 - q, W - 1:W], ALU.add, ALU.max).then_inc(fm_ready, 1)
            batches(dve, body)


def edge_softmax_phase(nc, C, A):
    B, W = EBATCH, ETILE
    ctx = ExitStack()
    with ctx:
        def sb(name, shape, dt=F32):
            return ctx.enter_context(nc.sbuf_tensor("ex_" + name, shape, dt))

        def sem(name):
            C.sems.append(ctx.enter_context(nc.semaphore("ex_" + name)))
            return C.sems[-1]

        dT = sb("dT", [HEADS, 2, W + 2], I32)
        al = sb("al", [HEADS, 2, W])
        fm = sb("fm", [HEADS, 2, W])
        v_sb = sb("v_sb", [P, 2, B, D])
        cut = sb("cut", [HEADS, 2, W])
        mx = sb("mx", [HEADS, 2, W])
        dif = sb("dif", [HEADS, 2, W])
        ex = sb("ex", [HEADS, 2, W])
        msg = sb("msg", [P, 2, B, D + HEADS])
        pe_x = ctx.enter_context(nc.psum_tensor("ex_pe", [P, B, HEADS], F32))
        rows_in = [sem("rows_in0"), sem("rows_in1")]
        stored = [sem("stored0"), sem("stored1")]
        cut_made, mx_ready, dif_ready, ex_ready = sem("cut_made"), sem("mx_ready"), sem("dif_ready"), sem("ex_ready")
        exT_ps, msg_ready = sem("exT_ps"), sem("msg_ready")
        paced = sem("paced")
        block = ctx.enter_context(nc.Block())

        @block.sync
        def _(sp):
            def load(i, q):
                n = 2 * i + q
                at = (ETILES - 1 - n) * W
                sp.dma_start(dT[:, q, :], A.dst_row[:, ds(at, W + 2)].partition_broadcast(HEADS)[:, 0, :])\
                    .then_inc(rows_in[q], 16)
                sp.dma_start(al[:, q, :], C.alphaT[:, ds(at, W)]).then_inc(rows_in[q], 16)
                sp.dma_start(fm[:, q, :], C.fmaxT[:, ds(at, W)]).then_inc(rows_in[q], 16)
                sp.dma_start(v_sb[:, q, :, :], C.v_e[ds(at, W), :].rearrange("(b p) f -> p b f", p=P))\
                    .then_inc(rows_in[q], 16)

            def store(i, q):
                n = 2 * i + q
                at = (ETILES - 1 - n) * W
                sp.wait_ge(msg_ready, n + 1)
                sp.sem_inc(paced, 1)
                sp.dma_start(C.msga[ds(at, W), :].rearrange("(b p) f -> p b f", p=P), msg[:, q, :, :])\
                    .then_inc(stored[q], 16)

            half = ETILES // 2
            load(0, 0)
            load(0, 1)
            with sp.Fori(0, half - 1) as i:
                store(i, 0)
                load(i + 1, 0)
                store(i, 1)
                load(i + 1, 1)
            store(half - 1, 0)
            load(half, 0)
            store(half - 1, 1)
            store(half, 0)
            sp.wait_ge(stored[0], 16 * (half + 1))
            sp.wait_ge(stored[1], 16 * half)

        @block.vector
        def _(dve):
            V = nc.vector

            def body(i, q, new, first):
                n = 2 * i + q
                dve.wait_ge(rows_in[q], 64 * (i + 1))
                V.tensor_tensor(cut[:, q, :], dT[:, q, 1:W + 1], dT[:, q, 2:W + 2], ALU.not_equal).then_inc(cut_made, 1)
                dve.wait_ge(cut_made, 2 * n + 1)
                V.tensor_scalar(cut[:, q, :], cut[:, q, :], -BIG, None, ALU.mult).then_inc(cut_made, 1)
                dve.wait_ge(cut_made, 2 * n + 2)
                if not first:
                    dve.wait_ge(mx_ready, n)
                V.tensor_tensor_scan(mx[:, q, ::-1], cut[:, q, ::-1], fm[:, q, ::-1],
                                     -BIG if first else mx[:, 1 - q, 0:1], ALU.add, ALU.max).then_inc(mx_ready, 1)
                dve.wait_ge(mx_ready, n + 1)
                V.tensor_tensor(dif[:, q, :], al[:, q, :], mx[:, q, :], ALU.subtract).then_inc(dif_ready, 1)
                dve.wait_ge(exT_ps, n + 1)
                if not new:
                    dve.wait_ge(stored[q], 16 * i)
                V.tensor_copy(msg[:, q, :, D:D + HEADS], pe_x[:, :, :])
                V.tensor_tensor(msg[:, q, :, 0:D].rearrange("p b (h c) -> p b h c", c=HC),
                                v_sb[:, q, :, :].rearrange("p b (h c) -> p b h c", c=HC),
                                pe_x[:, :, :].unsqueeze(3).to_broadcast([P, B, HEADS, HC]), ALU.mult)\
                    .then_inc(msg_ready, 1)
            batches(dve, body)

        @block.scalar
        def _(act):
            def body(i, q, new, first):
                n = 2 * i + q
                act.wait_ge(dif_ready, n + 1)
                nc.scalar.activation(ex[:, q, :], dif[:, q, :], ACT.Exp).then_inc(ex_ready, 1)
            batches(act, body)

        @block.tensor
        def _(pe):
            def body(i, q, new, first):
                n = 2 * i + q
                pe.wait_ge(ex_ready, n + 1)
                if not first:
                    pe.wait_ge(msg_ready, n)
                for j in range(B):
                    mm = nc.tensor.matmul(pe_x[:, j, :], ex[:, q, j * P:(j + 1) * P], C.ident[0:HEADS, 0:HEADS],
                                          start=True, stop=True)
                mm.then_inc(exT_ps, 1)
            batches(pe, body)


def ffn_phase(nc, C, A):
    ctx = ExitStack()
    FC = FF // P
    with ctx:
        def sb(name, shape, dt=F32):
            return ctx.enter_context(nc.sbuf_tensor("ff_" + name, shape, dt))

        def ps(name, shape):
            return ctx.enter_context(nc.psum_tensor("ff_" + name, shape, F32))

        def sem(name):
            C.sems.append(ctx.enter_context(nc.semaphore("ff_" + name)))
            return C.sems[-1]

        hl = sb("hl", [P, LAST])
        hT = sb("hT", [P, 2, TILE])
        x1 = sb("x1", [P, 2, NB, D])
        hn = sb("hn", [P, 2, TILE])
        g = sb("g", [P, 2, FC, TILE])
        y = sb("y", [P, 2, NB, D])
        x2 = sb("x2", [P, 2, NB, D])
        x2s = sb("x2s", [P, 2, NB, D])
        stats = sb("stats", [P, 2, NB, 6])
        mv = sb("mv", [P, 2, NB, 3])
        small = sb("small", [P, 2, 4, NB])
        gm = sb("gm", [P, 2])
        col = sb("col", [P, 8])
        half_pow = sb("half_pow", [P, NB])
        pf = [ps(f"pf{c}", [P, TILE]) for c in range(FC)]
        py = ps("py", [P, NB, D])

        hl_in, made, g_chain, root = sem("hl_in"), sem("made"), sem("g_chain"), sem("root")
        half_made = sem("half_made")
        hT_in = [sem("hT_in0"), sem("hT_in1")]
        x1_in = [sem("x1_in0"), sem("x1_in1")]
        x2_out = [sem("x2_out0"), sem("x2_out1")]
        hn_ready, f_ps, g_ready, y_ps = sem("hn_ready"), sem("f_ps"), sem("g_ready"), sem("y_ps")
        chain_s, root_s = sem("chain"), sem("root_s")
        x2_ready, x2s_ready = sem("x2_ready"), sem("x2s_ready")
        block = ctx.enter_context(nc.Block())
        LP = 6

        def tiles(eng, body):
            for q in range(2):
                body(0, q, True, q == 0, False)
            with eng.Fori(1, TILES // 2 - 1) as i:
                for q in range(2):
                    body(i, q, False, False, False)
            for q in range(2):
                body(TILES // 2 - 1, q, False, False, q == 1)

        @block.sync
        def _(sp):
            sp.dma_start(hl[:, :], C.hT[:, (TILES - 1) * TILE:N_NODES]).then_inc(hl_in, 16)

            def load_h(i, q):
                sp.dma_start(hT[:, q, :], C.hT[:, ds((2 * i + q) * TILE, TILE)]).then_inc(hT_in[q], 16)

            def load_x(i, q):
                sp.dma_start(x1[:, q, :, :], rows_tile(C.x1, 2 * i + q)).then_inc(x1_in[q], 16)

            for q in range(2):
                load_h(0, q)
                load_x(0, q)

            def body(i, q, new, first, last):
                t = 2 * i + q
                final = isinstance(i, int) and i == TILES // 2 - 1
                if not final:
                    sp.wait_ge(hn_ready, t + 1)
                    load_h(i + 1, q)
                    sp.wait_ge(chain_s, LP * t + 1)
                    load_x(i + 1, q)
                sp.wait_ge(x2_ready, t + 1)
                sp.dma_start(rows_tile(C.x2, t), x2[:, q, :, :]).then_inc(x2_out[q], 16)
                sp.wait_ge(x2s_ready, t + 1)
                sp.dma_start(rows_tile(C.x2s, t), x2s[:, q, :, :]).then_inc(x2_out[q], 16)
            tiles(sp, body)
            for q in range(2):
                sp.wait_ge(x2_out[q], 32 * (TILES // 2))

        @block.tensor
        def _(pe):
            T = nc.tensor

            def up(i, q, first):
                t = 2 * i + q
                pe.wait_ge(hn_ready, t + 1)
                for c in range(FC):
                    if not first:
                        pe.wait_ge(g_ready, FC * (t - 1) + c + 1)
                    T.matmul(pf[c][:, :], C.wf1[:, c * P:(c + 1) * P], hn[:, q, :], start=True, stop=True)\
                        .then_inc(f_ps, 1)

            def down(i, q, first):
                t = 2 * i + q
                if not first:
                    pe.wait_ge(chain_s, LP * (t - 1) + 1)
                pe.wait_ge(g_ready, FC * (t + 1))
                for b in range(NB):
                    o, w = BROW["ffn2"]
                    nodes = slice(b * P, (b + 1) * P)
                    T.matmul(py[:, b, :], C.ones3[:, :], C.bias3[:, o:o + w], start=True, stop=False)
                    T.matmul(py[:, b, :], hn[:, q, nodes], C.ident[:, :], start=False, stop=False)
                    for c in range(FC):
                        mm = T.matmul(py[:, b, :], g[:, q, c, nodes], C.wf2[:, c, :], start=False, stop=(c == FC - 1))
                mm.then_inc(y_ps, 1)

            up(0, 0, True)

            def body(i, q, new, first, last):
                if not last:
                    up(i + (q + 1) // 2, (q + 1) % 2, False)
                down(i, q, first)
            tiles(pe, body)

        @block.scalar
        def _(act):
            S = nc.scalar
            act.wait_ge(g_chain, 7)
            S.activation(col[:, 4:5], col[:, 3:4], ACT.Sqrt).then_inc(root, 1)

            def gelu(i, q, new):
                t = 2 * i + q
                if not new:
                    act.wait_ge(y_ps, t - 1)
                for c in range(FC):
                    act.wait_ge(f_ps, FC * t + c + 1)
                    S.activation(g[:, q, c, :], pf[c][:, :], ACT.Gelu, bias=C.bf1[:, c:c + 1]).then_inc(g_ready, 1)

            def rows(i, q, new):
                t = 2 * i + q
                act.wait_ge(chain_s, LP * (t + 1))
                if not new:
                    act.wait_ge(x2_out[q], 32 * i)
                    act.wait_ge(x2s_ready, t - 1)
                for b in range(NB):
                    ins = S.activation(x2[:, q, b, :], y[:, q, b, :], ACT.Identity,
                                       bias=small[:, q, 3, b:b + 1], scale=small[:, q, 2, b:b + 1])
                ins.then_inc(x2_ready, 1)

            gelu(0, 0, True)

            def body(i, q, new, first, last):
                if not last:
                    gelu(i + (q + 1) // 2, (q + 1) % 2, new and q == 0)
                rows(i, q, new)
            tiles(act, body)

        @block.vector
        def _(dve):
            V = nc.vector
            a = Chain(dve, g_chain, 9)
            a.begin(0)
            dve.wait_ge(hl_in, 16)
            a.link(V.bn_stats(C.gstats[:, 6 * (TILES - 1):6 * TILES], hl[:, :]))
            a.link(V.bn_aggr(gm[:, :], C.gstats[:, :]))
            a.link(V.tensor_tensor(col[:, 0:1], gm[:, 0:1], C.gnms[:, :], ALU.mult))
            a.link(V.tensor_tensor(col[:, 1:2], gm[:, 0:1], col[:, 0:1], ALU.subtract))
            a.link(V.tensor_tensor(col[:, 2:3], col[:, 1:2], col[:, 1:2], ALU.mult))
            a.link(V.tensor_tensor(col[:, 2:3], col[:, 2:3], gm[:, 1:2], ALU.add))
            a.link(V.tensor_scalar(col[:, 3:4], col[:, 2:3], EPS, None, ALU.add))
            dve.wait_ge(root, 1)
            a.link(V.reciprocal(col[:, 5:6], col[:, 4:5]))
            a.link(V.tensor_tensor(col[:, 5:6], col[:, 5:6], C.gnw[:, :], ALU.mult))
            V.scalar_tensor_tensor(col[:, 7:8], col[:, 0:1], -1.0, col[:, 5:6], ALU.mult, ALU.mult).then_inc(made, 1)
            dve.wait_ge(made, 1)
            V.tensor_tensor(col[:, 6:7], col[:, 7:8], C.gnb[:, :], ALU.add).then_inc(made, 1)
            dve.wait_ge(made, 2)

            def normed(i, q):
                dve.wait_ge(hT_in[q], 16 * (i + 1))
                V.tensor_scalar(hn[:, q, :], hT[:, q, :], col[:, 5:6], col[:, 6:7], ALU.mult, ALU.add)\
                    .then_inc(hn_ready, 1)

            p = Chain(dve, chain_s, LP)
            normed(0, 0)
            normed(0, 1)

            def body(i, q, new, first, last):
                t = 2 * i + q
                p.begin(t)
                dve.wait_ge(y_ps, t + 1)
                if not (isinstance(i, int) and i == TILES // 2 - 1):
                    normed(i + 1, q)
                dve.wait_ge(x1_in[q], 16 * (i + 1))
                if not new:
                    dve.wait_ge(x2_ready, t - 1)
                p.link(V.tensor_tensor(y[:, q, :, :], py[:, :, :], x1[:, q, :, :], ALU.add))
                for b in range(NB):
                    ins = V.bn_stats(stats[:, q, b, :], y[:, q, b, :])
                p.link(ins)
                row_variance(V, p, stats[:, q, :, :], mv[:, q, :, :], small[:, q, 0, :])
                dve.wait_ge(root_s, t + 1)
                p.mark(V.scalar_tensor_tensor(small[:, q, 3, :], mv[:, q, :, 0], -0.5, small[:, q, 2, :],
                                              ALU.mult, ALU.mult))
            tiles(dve, body)

        @block.gpsimd
        def _(pool):
            nc.gpsimd.memset(half_pow[:, :], -0.5).then_inc(half_made, 1)
            pool.wait_ge(half_made, 1)

            def scaled(i, q, new):
                t = 2 * i + q
                pool.wait_ge(x2_ready, t + 1)
                if not new:
                    pool.wait_ge(x2_out[q], 32 * i)
                nc.gpsimd.tensor_tensor(x2s[:, q, :, :], x2[:, q, :, :],
                                        C.dinv[:, ds(NB * t, NB)].unsqueeze(2).to_broadcast([P, NB, D]), ALU.mult)\
                    .then_inc(x2s_ready, 1)

            def body(i, q, new, first, last):
                t = 2 * i + q
                pool.wait_ge(chain_s, LP * t + 5)
                if not new:
                    pool.wait_ge(x2_ready, t - 1)
                nc.gpsimd.tensor_tensor(small[:, q, 2, :], small[:, q, 0, :], half_pow[:, :], ALU.pow)\
                    .then_inc(root_s, 1)
                scaled(i, q, new)
            tiles(pool, body)


def clear_semaphores(nc, sems):
    nums = sorted(s.num for s in sems)
    with nc.Block() as block:
        @block.sync
        def _(sp):
            at = 0
            for n in range(1, len(nums) + 1):
                if n == len(nums) or nums[n] != nums[n - 1] + 1:
                    sp.sem_clear(range(nums[at], nums[n - 1] + 1))
                    at = n


def build(nc, A, out):
    ctx = ExitStack()
    C = Names()
    with ctx:
        def keep(name, shape, dt=F32):
            return ctx.enter_context(nc.sbuf_tensor("c_" + name, shape, dt))

        C.src_sb, C.dst_sb = keep("src", [P, EB], I32), keep("dst", [P, EB], I32)
        for name in ("w1l", "w1r", "w2l", "w2r", "wq", "wk", "wv", "wp", "wo_bc", "bl_bc", "ident"):
            C[name] = keep(name, [P, D])
        C.wek, C.wev = keep("wek", [11, D]), keep("wev", [11, D])
        C.wsk = keep("wsk", [P, D + 1])
        C.bq, C.gnw, C.gnb, C.gnms = (keep(n, [P, 1]) for n in ("bq", "gnw", "gnb", "gnms"))
        C.wf1, C.bf1, C.wf2 = keep("wf1", [P, FF]), keep("bf1", [P, FF // P]), keep("wf2", [P, FF // P, D])
        C.wg0, C.wg1, C.wgl = keep("wg0", [P, HID]), keep("wg1", [P, 2, HID]), keep("wgl", [P, 2, D])
        C.headw = keep("headw", [P, HEADS])
        C.iota = keep("iota", [P, TILE])
        C.gate, C.gate_out = keep("gate", [P, 1]), keep("gate_out", [P, 4])
        C.ones3, C.bias3 = keep("ones3", [3, P], BF16), keep("bias3", [3, BROWS], BF16)
        C.ext = keep("ext", [P, EB, 3])
        C.keep, C.base = keep("keep", [P, STEPS]), keep("base", [P, STEPS])
        C.meta, C.trips = keep("meta", [1, META * STEPS], I32), keep("trips", [1, 2], I32)
        C.dst_tab, C.w_tab = keep("dst_tab", [P, NB * STEPS]), keep("w_tab", [P, NB * STEPS])
        C.inv_cnt, C.deg, C.dinv = (keep(n, [P, NB * TILES]) for n in ("inv_cnt", "deg", "dinv"))
        C.gstats = keep("gstats", [P, 6 * TILES])

        def scratch(name, shape):
            return nc.dram_tensor("scratch_" + name, shape, F32, kind="Internal").ap()

        C.bounce = scratch("bounce", (7, STEPS))
        C.msgx, C.msg = scratch("msgx", (EROWS, 131)), scratch("msg", (EROWS, D))
        C.msga, C.msg2 = scratch("msga", (EROWS, D + HEADS)), scratch("msg2", (EROWS, HID))
        C.h, C.x1, C.x2, C.x2s, C.z, C.x3 = (scratch(n, (NODES, D)) for n in ("h", "x1", "x2", "x2s", "z", "x3"))
        C.g1s = scratch("g1s", (NODES, HID))
        C.hT = scratch("hT", (D, NODES))
        C.v_e = scratch("v_e", (EDGES, D))
        C.alphaT, C.fmaxT = scratch("alphaT", (HEADS, EDGES)), scratch("fmaxT", (HEADS, EDGES))

        stages = [
            lambda: setup_phase(nc, C, A),
            lambda: conv_phase(nc, C, "sage1", A.x, C.msgx, (A.x,), C.h),
            lambda: conv_phase(nc, C, "sage2", C.h, C.msg, (C.h, A.x), C.x1),
            lambda: edge_scores_phase(nc, C, A),
            lambda: edge_softmax_phase(nc, C, A),
            lambda: conv_phase(nc, C, "attn", None, C.msga, (C.x1,), C.hT),
            lambda: ffn_phase(nc, C, A),
            lambda: conv_phase(nc, C, "gcn1", C.x2s, C.msg, (C.x2s,), C.g1s),
            lambda: conv_phase(nc, C, "gcn2", C.g1s, C.msg2, (C.g1s,), C.z),
            lambda: conv_phase(nc, C, "gcn3", C.z, C.msg, (C.z, C.x2), C.x3),
            lambda: conv_phase(nc, C, "pool", C.x3, C.msg, (C.x3,), out),
        ]
        for name in ("gathered", "rows_in"):
            C[name] = {
                kind: [ctx.enter_context(nc.semaphore(f"{kind}_{name}{q}")) for q in range(2)]
                for kind in (*(k for k in KINDS if KINDS[k]["F"]), "scores")}
        for stage in stages:
            C.sems = []
            stage()
            clear_semaphores(nc, C.sems)


def layout(inputs):
    import numpy as np

    g = {k: np.asarray(v) for k, v in inputs.items()}

    def cols(v, fill):
        v = np.concatenate([v, np.full(EDGES - N_EDGES, fill, v.dtype)])
        return np.ascontiguousarray(v.reshape(EB, P).T)

    pad_node = NODES - 1
    no_node = np.full(1, -1, g["dst"].dtype)
    a = {
        "x": np.concatenate([g["x"], np.zeros((NODES - N_NODES, D), np.float32)]),
        "src_cols": cols(g["src"], 0),
        "dst_cols": cols(g["dst"], pad_node),
        "w_cols": cols(g["edge_weight"], 0),
        "dst_row": np.concatenate([no_node, g["dst"], np.full(EDGES - N_EDGES, pad_node, g["dst"].dtype), no_node])[None],
        "ea_rows": np.concatenate([g["edge_attr_10"].T, np.zeros((10, EDGES - N_EDGES), np.float32)], axis=1),
        "W1lT": g["L0_gnn_W1_l"].T, "W1rT": g["L0_gnn_W1_r"].T,
        "W2lT": g["L0_gnn_W2_l"].T, "W2rT": g["L0_gnn_W2_r"].T,
        "b1l": g["L0_gnn_b1_l"][None], "b2l": g["L0_gnn_b2_l"][None],
        "Wq": g["L1_gnn_Wq"], "Wk": g["L1_gnn_Wk"], "Wv": g["L1_gnn_Wv"], "We": g["L1_gnn_We"],
        "bq": g["L1_gnn_bq"][:, None], "bk": g["L1_gnn_bk"][None], "bv": g["L1_gnn_bv"][None],
        "Wskip": g["L1_gnn_Wskip"], "WskipT": g["L1_gnn_Wskip"].T,
        "bskip": g["L1_gnn_bskip"][None], "bskip_col": g["L1_gnn_bskip"][:, None],
        "wbeta_a": g["L1_gnn_Wbeta"][0:D, 0][None], "wbeta_c": g["L1_gnn_Wbeta"][2 * D:3 * D, 0][None],
        "wbeta_b_col": g["L1_gnn_Wbeta"][D:2 * D], "wbeta_c_col": g["L1_gnn_Wbeta"][2 * D:3 * D],
        "gn_w": g["L1_gnn_gn_w"][:, None], "gn_b": g["L1_gnn_gn_b"][:, None], "gn_ms": g["L1_gnn_gn_ms"][:, None],
        "fW1": g["L1_gnn_W1"], "fb1": g["L1_gnn_b1"].reshape(FF // P, P).T, "fW2": g["L1_gnn_W2"],
        "fb2": g["L1_gnn_b2"][None],
        "gW0": g["L2_gnn_W0"], "gW1": g["L2_gnn_W1"], "gWl": g["L2_gnn_Wl"], "gbl": g["L2_gnn_bl"][None],
        "gb0": g["L2_gnn_b0"][None], "gb1": g["L2_gnn_b1"][None],
        "gbe0": g["L2_gnn_be0"][None], "gbe1": g["L2_gnn_be1"][None],
        "gg0": g["L2_gnn_g0"][None], "gg1": g["L2_gnn_g1"][None],
        "pW": g["L3_gnn_W"], "pb": g["L3_gnn_b"][None],
    }
    return {k: np.ascontiguousarray(v) for k, v in a.items()}


def kernel(**inputs):
    import numpy as np
    import concourse.bacc as bacc
    from concourse.bass_utils import run_bass_kernel_spmd

    nc = bacc.Bacc("TRN2", target_bir_lowering=False, num_devices=1)
    arrays = layout(inputs)
    A = Names(**{
        name: nc.dram_tensor("in_" + name, a.shape, mybir.dt.from_np(a.dtype), kind="ExternalInput").ap()
        for name, a in arrays.items()})
    out = nc.dram_tensor("out_x", (NODES, D), F32, kind="ExternalOutput").ap()
    build(nc, A, out)
    r = run_bass_kernel_spmd(nc, [{"in_" + name: a for name, a in arrays.items()}], core_ids=[0])
    return np.asarray(r.results[0]["out_x"])[:N_NODES]
```
